# Optimizing a Trainium2 kernel written in Bass

```python
import numpy as np
import jax
import jax.numpy as jnp

def _softmax(x, axis=-1):
    return jax.nn.softmax(x, axis=axis)

def _gelu(x):
    return jax.nn.gelu(x, approximate=True)

def _silu(x):
    return jax.nn.silu(x)

def _sigmoid(x):
    return jax.nn.sigmoid(x)

def _layernorm(x, axis=-1, eps=1e-05):
    m = jnp.mean(x, axis=axis, keepdims=True)
    v = jnp.var(x, axis=axis, keepdims=True)
    return (x - m) / jnp.sqrt(v + eps)

def _scatter_add(tgt, idx, src, axis=0):
    return tgt.at[idx].add(src)

def _segment_sum(src, seg, n):
    return jax.ops.segment_sum(src, seg, n)
kernel_name = 'mk_gnn_preln_d2_gnn_r8_3df9b3'

def setup_inputs(seed: int=0):
    np.random.seed(seed)
    _w = jnp.asarray

    def _rec_inputs():
        import jax
        import jax.numpy as jnp
        _gk = jax.random.key(seed)
        x = -0.000202 + 1 * jax.random.normal(jax.random.fold_in(_gk, 1), (6250, 128), jnp.float32)
        _s = jax.random.randint(jax.random.fold_in(_gk, 2), (50000,), 0, 6250, jnp.int32)
        _d = jax.random.randint(jax.random.fold_in(_gk, 3), (50000,), 0, 6250, jnp.int32)
        _loop = jnp.arange(6250, dtype=jnp.int32)
        src = jnp.concatenate([_s, _d, _loop])
        dst = jnp.concatenate([_d, _s, _loop])
        _o = jnp.argsort(dst, stable=True)
        src = src[_o]
        dst = dst[_o]
        edge_attr_128 = 2.93046e-05 + 1.00006 * jax.random.normal(jax.random.fold_in(_gk, 11), (106250, 128), jnp.float32)
        return (x, src, dst, edge_attr_128)
    x, src, dst, edge_attr_128 = _rec_inputs()

    def _L0_gnn_setup():
        import jax, jax.numpy as jnp
        import numpy as np
        N = 6250
        E = 100000
        D = 128

        def _sage_conv(x, src, dst, W_l, b_l, W_r):
            msg_sum = jax.ops.segment_sum(x[src], dst, num_segments=N)
            deg = jax.ops.segment_sum(jnp.ones((src.shape[0],), x.dtype), dst, num_segments=N)
            agg = msg_sum / jnp.maximum(deg, 1.0)[:, None]
            return agg @ W_l.T + b_l + x @ W_r.T
        key = jax.random.key(seed)
        ks = jax.random.split(key, 12)
        s = 1.0 / np.sqrt(D)
        inp = {'x': jax.random.normal(ks[0], (N, D), dtype=jnp.float32), 'edge_index': jax.random.randint(ks[1], (2, E), 0, N, dtype=jnp.int64)}
        for i in (1, 2, 3):
            inp[f'W_l{i}'] = jax.random.uniform(ks[3 * i - 1], (D, D), jnp.float32, -s, s)
            inp[f'b_l{i}'] = jax.random.uniform(ks[3 * i], (D,), jnp.float32, -s, s)
            inp[f'W_r{i}'] = jax.random.uniform(ks[3 * i + 1], (D, D), jnp.float32, -s, s)
        return inp
    _L0_gnn_all = _L0_gnn_setup()
    _L0_gnn_in = {k: v for k, v in _L0_gnn_all.items() if k in ('W_l1', 'b_l1', 'W_r1', 'W_l2', 'b_l2', 'W_r2', 'W_l3', 'b_l3', 'W_r3')}
    del _L0_gnn_all

    def _L1_gnn_setup():
        import jax, jax.numpy as jnp
        import numpy as np
        N = 5000
        E = 80000
        D = 128
        key = jax.random.key(seed)
        ks = jax.random.split(key, 9)
        s2 = 1.0 / np.sqrt(2 * D)
        s1 = 1.0 / np.sqrt(D)
        return {'nodes': jax.random.normal(ks[0], (N, D), jnp.float32), 'edge_index': jax.random.randint(ks[1], (2, E), 0, N, jnp.int32), 'edge_features': jax.random.normal(ks[2], (E, D), jnp.float32), 'mw1': jax.random.uniform(ks[3], (2 * D, D), jnp.float32, -s2, s2), 'mb1': jax.random.uniform(ks[4], (D,), jnp.float32, -s2, s2), 'uw1': jax.random.uniform(ks[5], (2 * D, D), jnp.float32, -s2, s2), 'ub1': jax.random.uniform(ks[6], (D,), jnp.float32, -s2, s2), 'uw2': jax.random.uniform(ks[7], (D, D), jnp.float32, -s1, s1), 'ub2': jax.random.uniform(ks[8], (D,), jnp.float32, -s1, s1)}
    _L1_gnn_all = _L1_gnn_setup()
    _L1_gnn_in = {k: v for k, v in _L1_gnn_all.items() if k in ('mw1', 'mb1', 'uw1', 'ub1', 'uw2', 'ub2')}
    del _L1_gnn_all
    return {'x': x, 'src': src, 'dst': dst, 'edge_attr_128': edge_attr_128, 'L0_gnn_W_l1': _L0_gnn_in['W_l1'], 'L0_gnn_b_l1': _L0_gnn_in['b_l1'], 'L0_gnn_W_r1': _L0_gnn_in['W_r1'], 'L0_gnn_W_l2': _L0_gnn_in['W_l2'], 'L0_gnn_b_l2': _L0_gnn_in['b_l2'], 'L0_gnn_W_r2': _L0_gnn_in['W_r2'], 'L0_gnn_W_l3': _L0_gnn_in['W_l3'], 'L0_gnn_b_l3': _L0_gnn_in['b_l3'], 'L0_gnn_W_r3': _L0_gnn_in['W_r3'], 'L1_gnn_mw1': _L1_gnn_in['mw1'], 'L1_gnn_mb1': _L1_gnn_in['mb1'], 'L1_gnn_uw1': _L1_gnn_in['uw1'], 'L1_gnn_ub1': _L1_gnn_in['ub1'], 'L1_gnn_uw2': _L1_gnn_in['uw2'], 'L1_gnn_ub2': _L1_gnn_in['ub2']}

def reference(x, src, dst, edge_attr_128, L0_gnn_W_l1, L0_gnn_b_l1, L0_gnn_W_r1, L0_gnn_W_l2, L0_gnn_b_l2, L0_gnn_W_r2, L0_gnn_W_l3, L0_gnn_b_l3, L0_gnn_W_r3, L1_gnn_mw1, L1_gnn_mb1, L1_gnn_uw1, L1_gnn_ub1, L1_gnn_uw2, L1_gnn_ub2):
    import jax
    import jax.numpy as jnp

    def _L0_gnn_ref(x, edge_index, W_l1, b_l1, W_r1, W_l2, b_l2, W_r2, W_l3, b_l3, W_r3):
        import jax, jax.numpy as jnp
        import numpy as np
        N = 6250
        E = 100000
        D = 128

        def _sage_conv(x, src, dst, W_l, b_l, W_r):
            msg_sum = jax.ops.segment_sum(x[src], dst, num_segments=N)
            deg = jax.ops.segment_sum(jnp.ones((src.shape[0],), x.dtype), dst, num_segments=N)
            agg = msg_sum / jnp.maximum(deg, 1.0)[:, None]
            return agg @ W_l.T + b_l + x @ W_r.T
        src, dst = (edge_index[0], edge_index[1])
        h1 = jax.nn.relu(_sage_conv(x, src, dst, W_l1, b_l1, W_r1))
        h2 = jax.nn.relu(_sage_conv(h1, src, dst, W_l2, b_l2, W_r2))
        h2 = h2 + h1
        out = _sage_conv(h2, src, dst, W_l3, b_l3, W_r3)
        return out

    def _L1_gnn_ref(nodes, edge_index, edge_features, mw1, mb1, uw1, ub1, uw2, ub2):
        import jax, jax.numpy as jnp
        import numpy as np
        N = 5000
        E = 80000
        D = 128
        src, dst = (edge_index[0], edge_index[1])
        msg_in = jnp.concatenate([nodes[src], edge_features], axis=1)
        messages = jax.nn.silu(msg_in @ mw1 + mb1)
        aggregated = jax.ops.segment_sum(messages, dst, num_segments=nodes.shape[0])
        upd_in = jnp.concatenate([nodes, aggregated], axis=1)
        updated = jax.nn.silu(upd_in @ uw1 + ub1) @ uw2 + ub2
        return nodes + updated
    edge_index = jnp.stack([src, dst])
    h = jnp.maximum(_layernorm(x, axis=-1), 0.0)
    x = x + _L0_gnn_ref(h, edge_index, L0_gnn_W_l1, L0_gnn_b_l1, L0_gnn_W_r1, L0_gnn_W_l2, L0_gnn_b_l2, L0_gnn_W_r2, L0_gnn_W_l3, L0_gnn_b_l3, L0_gnn_W_r3)
    h = jnp.maximum(_layernorm(x, axis=-1), 0.0)
    x = x + _L1_gnn_ref(h, edge_index, edge_attr_128, L1_gnn_mw1, L1_gnn_mb1, L1_gnn_uw1, L1_gnn_ub1, L1_gnn_uw2, L1_gnn_ub2)
    return x

_drawn_inputs = setup_inputs


def setup_inputs(seed=0):
    import zlib

    import numpy as np

    out = dict(_drawn_inputs(seed))
    spreads = {}
    factors = {'L1_gnn_ub1': 6.032}
    for name, (base, spread) in spreads.items():
        noise = np.random.default_rng([zlib.crc32(name.encode()), seed]).standard_normal(out[name].shape)
        drawn = base * np.exp(spread * noise) if base else spread * noise
        out[name] = jnp.asarray(drawn.astype(out[name].dtype))
    for name, factor in factors.items():
        out[name] = (out[name] * factor).astype(out[name].dtype)
    return out
```

```python
from contextlib import ExitStack

import concourse.bass as bass
from concourse import mybir

F32 = mybir.dt.float32
I32 = mybir.dt.int32
U32 = mybir.dt.uint32
ALU = mybir.AluOpType
ACT = mybir.ActivationFunctionType
AX_X = mybir.AxisListType.X

P = 128
N = 6250
D = 128
E = 106250
EPS = 1e-5

CH = 512
JC = CH // P
NCH = -(-N // CH)
NP = NCH * CH

BT = 4
W = 64
BODY = 16
NK = BODY // BT
HALF = BODY // 2
NTURN = -(-E // (P * BODY))
NT = NTURN * BODY
NB = NT // BT
EP = NT * P
PAD_DST = 8191
assert PAD_DST >= NP + W and NCH % 2 == 1


def after(eng, sem, value):
    if not isinstance(value, int) or value > 0:
        eng.wait_ge(sem, value)


def turns(eng):
    yield 0
    with eng.Fori(1, NTURN) as i:
        yield i


def chunks(eng):
    yield 0, 0, 0
    yield 1, 1, 1 - 1
    with eng.Fori(1, NCH // 2) as i:
        yield 2 * i, 0, i
        yield 2 * i + 1, 1, i
    yield NCH - 1, 0, NCH // 2


def gnn_kernel(nc, x, src_t, dst_t, dst_first, edge_T, WlT, bl, WrT, mw1, mb1, uw1, ub1, uw2, ub2, out):
    with ExitStack() as ctx:
        def sb(name, shape, dt=F32):
            return ctx.enter_context(nc.sbuf_tensor(name, shape, dt))

        def sem(name):
            return ctx.enter_context(nc.semaphore(name))

        bank = [ctx.enter_context(nc.psum_tensor(f"bank{b}", [P, 512], F32)) for b in range(8)]
        table = [nc.dram_tensor(f"table{l}", [NP, D], F32).ap() for l in range(4)]

        ident = sb("ident", [P, P])
        ones = sb("ones", [P, P])
        iota_i = sb("iota_i", [P, CH], I32)
        iota_f = sb("iota_f", [P, CH])
        wl = sb("wl", [P, 3, D])
        wr = sb("wr", [P, 3, D])
        mw = sb("mw", [P, 2, D])
        uw = sb("uw", [P, 2, D])
        uw2_sb = sb("uw2_sb", [P, D])
        bcol = sb("bcol", [P, 4])
        mb1_row = sb("mb1_row", [P, D])
        ub2_row = sb("ub2_row", [P, D])
        eps_col = sb("eps_col", [P, 1])

        src_sb = sb("src_sb", [P, NT], I32)
        dst_i = sb("dst_i", [P, NT], I32)
        first_row = sb("first_row", [1, NB], I32)
        first_i = sb("first_i", [P, NB], I32)
        rel = sb("rel", [P, NB, BT])
        left = sb("left", [P, NT])
        left_n = sb("left_n", [P, 1])
        left_flag = sb("left_flag", [P, 1], I32)

        hT = sb("hT", [P, NP])
        acc = sb("acc", [P, 2, NP])

        idx = sb("idx", [P, 2, HALF], I32)
        gath = sb("gath", [P, BODY, D])
        onehot = sb("onehot", [P, NK, BT, W])
        efT = sb("efT", [P, 2, HALF * P])
        pre = sb("pre", [P, 2, BT * D])
        msg = sb("msg", [P, 2, BT, D])
        idx_left = sb("idx_left", [P, 1], I32)
        gath_left = sb("gath_left", [P, D])
        ef_left = sb("ef_left", [P, P])
        pre_left = sb("pre_left", [P, D])
        msg_left = sb("msg_left", [P, D])
        hot_left = sb("hot_left", [P, CH])

        xin = sb("xin", [P, 2, JC, D])
        stats = sb("stats", [P, 2, JC, 6])
        meanvar = sb("meanvar", [P, 2, JC, 2])
        std = sb("std", [P, 2, JC])
        rstd = sb("rstd", [P, 2, JC])
        y = sb("y", [P, 2, JC, D])
        hn = sb("hn", [P, 2, JC, D])
        agg = sb("agg", [P, 2, CH])
        z = sb("z", [P, 2, CH])
        z2 = sb("z2", [P, 2, CH])
        rows = sb("rows", [P, 2, JC, D])
        x1 = sb("x1", [P, 2, JC, D])

        consts_in = sem("consts_in")
        passed = sem("passed")
        edges_in = sem("edges_in")
        const_built = sem("const_built")
        prep = sem("prep")
        left_sum = sem("left_sum")
        flag_ready = sem("flag_ready")
        idx_ready = sem("idx_ready")
        gathered = [sem(f"gathered{s}") for s in range(BODY)]
        onehot_ready = sem("onehot_ready")
        block_summed = sem("block_summed")
        added = sem("added")
        ef_in = [sem("ef_in0"), sem("ef_in1")]
        edge_mm = sem("edge_mm")
        pre_ready = sem("pre_ready")
        msg_ready = sem("msg_ready")
        acc_zeroed = sem("acc_zeroed")
        degree_ready = sem("degree_ready")
        out_written = [sem("out_written0"), sem("out_written1")]
        table_in = [[sem(f"table_in{l}_{q}") for q in range(2)] for l in range(4)]
        NAMES = ["x_in0", "x_in1", "stats_ready", "var_ready", "std_ready", "rstd_ready", "y_ready", "hn_ready",
                 "turned", "hT_ready", "agg_ready", "z_mm", "z_ready", "res_ready", "turned2", "rows_ready",
                 "x1_ready", "z2_ready", "row_mm", "kept_part"]
        USED = [NAMES[0:10] ,
                ["agg_ready", "z_mm", "z_ready", "turned", "hT_ready", "rows_ready"],
                ["agg_ready", "z_mm", "z_ready", "res_ready", "turned", "hT_ready", "rows_ready"],
                NAMES,
                ["z_mm", "z_ready", "row_mm", "rows_ready"]]
        st = [{n: sem(f"n{k}_{n}") for n in names} for k, names in enumerate(USED)]
        LEFT = ["idx", "gathered", "ef_in", "edge_mm", "pre", "msg", "onehot", "summed", "added"]
        lf = [{n: sem(f"left{l}_{n}") for n in LEFT[:2] + LEFT[6:] + (LEFT[2:6] if l == 3 else [])} for l in range(4)]

        N_CONST = 14

        def apart(eng):
            eng.sem_inc(passed, 1)

        chunk_of = lambda c: bass.ds(c * CH, CH)
        x_v = x.rearrange("(c j p) d -> c p j d", p=P, j=JC)
        out_v = out.rearrange("(c j p) d -> c p j d", p=P, j=JC)
        table_v = [t.rearrange("(c j p) d -> c p j d", p=P, j=JC) for t in table]
        pT = lambda b: bank[b][:, :].rearrange("p (j d) -> p j d", j=JC)

        def wide(row):
            return row[:, :].rearrange("p (o d) -> p o d", o=1).to_broadcast([P, JC, D])

        block = ctx.enter_context(nc.Block())

        @block.sync
        def _(sp):
            loads = [(wl[:, :, :], WlT), (wr[:, :, :], WrT), (mw[:, :, :], mw1.rearrange("(t k) m -> k t m", t=2)),
                     (uw[:, :, :], uw1.rearrange("(t k) m -> k t m", t=2)), (uw2_sb[:, :], uw2),
                     (mb1_row[:, :], mb1.rearrange("(o d) -> o d", o=1).to_broadcast([P, D])),
                     (ub2_row[:, :], ub2.rearrange("(o d) -> o d", o=1).to_broadcast([P, D])),
                     (first_i[:, :], dst_first.to_broadcast([P, NB])),
                     (first_row[:, :], dst_first), (dst_i[:, :], dst_t), (src_sb[:, :], src_t)]
            sp.dma_start(dst_i[:, :], dst_t).then_inc(edges_in, 16)
            sp.dma_start(first_i[:, :], dst_first.to_broadcast([P, NB])).then_inc(edges_in, 16)
            sp.dma_start(first_row[:, :], dst_first).then_inc(edges_in, 16)
            sp.dma_start(src_sb[:, :], src_t).then_inc(edges_in, 16)

            def load_x(s, c, q, u):
                after(sp, s["y_ready"] if s is st[0] else s["x1_ready"], c - 1)
                sp.dma_start(xin[:, q], x_v[c]).then_inc(s[f"x_in{q}"], 16)

            s = st[0]
            for c, q, u in chunks(sp):
                load_x(s, c, q, u)
                if isinstance(c, int) and c == 0:
                    for to, of in loads[:7]:
                        sp.dma_start(to, of).then_inc(consts_in, 16)
                    for k in range(4):
                        b = ub1 if k == 3 else bl[k]
                        sp.dma_start(bcol[:, k:k + 1], b.rearrange("(d o) -> d o", o=1)).then_inc(consts_in, 16)
                sp.wait_ge(s["hn_ready"], c + 1)
                sp.dma_start(table_v[0][c], hn[:, q]).then_inc(table_in[0][q], 16)

            def left_loads(l):
                s = lf[l]
                with sp.Fori(0, NT) as t:
                    sp.wait_ge(s["added"], NCH * t + 1)
                    apart(sp)
                    sp.dma_start(idx_left[:, :], src_t[:, bass.ds(t, 1)],
                                 allow_slow_non_contiguous=True).then_inc(s["idx"], 16)
                    if l == 3:
                        sp.dma_start(ef_left[:, :], edge_T[:, bass.ds(t * P, P)]).then_inc(s["ef_in"], 16)

            for l in range(4):
                if l == 3:
                    for i in turns(sp):
                        for q in range(2):
                            after(sp, edge_mm, NK * (i - 1) + NK // 2 * (q + 1))
                            sp.dma_start(efT[:, q], edge_T[:, bass.ds((i * 2 + q) * HALF * P, HALF * P)]).then_inc(ef_in[q], 16)
                sp.wait_ge(flag_ready, 1)
                n_left = sp.value_load(left_flag[0:1, 0:1], min_val=0, max_val=EP)
                with sp.If(n_left > 0):
                    left_loads(l)
                if l < 3:
                    s = st[l + 1]
                    for c, q, u in chunks(sp):
                        if l == 2:
                            load_x(s, c, q, u)
                        sp.wait_ge(s["rows_ready"], c + 1)
                        sp.dma_start(table_v[l + 1][c], rows[:, q]).then_inc(table_in[l + 1][q], 16)
            s = st[4]
            for c, q, u in chunks(sp):
                sp.wait_ge(s["rows_ready"], c + 1)
                sp.dma_start(out_v[c], rows[:, q]).then_inc(out_written[q], 16)
            sp.wait_ge(out_written[0], 16 * (NCH // 2 + 1))
            sp.wait_ge(out_written[1], 16 * (NCH // 2))

        @block.gpsimd
        def _(pool):
            nc.gpsimd.memset(ident[:, :], 0.0).then_inc(const_built, 1)
            nc.gpsimd.memset(ones[:, :], 1.0).then_inc(const_built, 1)
            nc.gpsimd.memset(eps_col[:, :], EPS).then_inc(const_built, 1)
            nc.gpsimd.iota(iota_i[:, :], pattern=[[1, CH]], base=0, channel_multiplier=0).then_inc(const_built, 1)
            pool.wait_ge(const_built, 4)
            nc.gpsimd.affine_select(out=ident[:, :], in_=ident[:, :], compare_op=ALU.not_equal, fill=1.0, base=0,
                                    pattern=[[-1, P]], channel_multiplier=1).then_inc(const_built, 1)

            for l in range(4):
                pool.wait_ge(table_in[l][0], 16 * (NCH // 2 + 1))
                pool.wait_ge(table_in[l][1], 16 * (NCH // 2))
                for i in turns(pool):
                    for t in range(BODY):
                        if t % HALF == 0:
                            pool.wait_ge(idx_ready, 2 * (NTURN * l + i) + t // HALF + 1)
                        if t % BT == 0:
                            if l < 3:
                                after(pool, block_summed, NK * (NTURN * l + i - 1) + t // BT + 1)
                            else:
                                after(pool, pre_ready, NK * (i - 1) + t // BT + 1)
                            apart(pool)
                        pool.indirect_dma_start(
                            out=gath[:, t, :], out_offset=None, in_=table[l],
                            in_offset=bass.IndirectOffsetOnAxis(ap=idx[:, t // HALF, t % HALF:t % HALF + 1].bitcast(U32), axis=0),
                        ).then_inc(gathered[t], 16)
                pool.wait_ge(flag_ready, 1)
                n_left = pool.value_load(left_flag[0:1, 0:1], min_val=0, max_val=EP)
                with pool.If(n_left > 0):
                    s = lf[l]
                    with pool.Fori(0, NT) as t:
                        pool.wait_ge(s["idx"], 16 * t + 16)
                        apart(pool)
                        pool.indirect_dma_start(
                            out=gath_left[:, :], out_offset=None, in_=table[l],
                            in_offset=bass.IndirectOffsetOnAxis(ap=idx_left[:, 0:1].bitcast(U32), axis=0),
                        ).then_inc(s["gathered"], 16)

        @block.scalar
        def _(act):
            act.wait_ge(const_built, 5)

            def ln_part(s, c, q):
                act.wait_ge(s["var_ready"], c + 1)
                nc.scalar.activation(std[:, q, :], meanvar[:, q, :, 1], ACT.Sqrt, bias=eps_col[:, 0:1]).then_inc(s["std_ready"], 1)
                act.wait_ge(s["y_ready"], c + 1)
                after(act, s["turned2"] if s is st[3] else s["turned"], c - 1)

            s = st[0]
            for c, q, u in chunks(act):
                ln_part(s, c, q)
                after(act, table_in[0][q], 16 * u)
                nc.scalar.activation(hn[:, q], y[:, q], ACT.Relu).then_inc(s["hn_ready"], 1)

            act.wait_ge(edges_in, 64)
            act.wait_ge(consts_in, 16 * 11)
            for l in range(4):
                for i in turns(act):
                    for q in range(2):
                        if isinstance(i, int) and l:
                            for t in range(HALF * q, HALF * (q + 1)):
                                act.wait_ge(gathered[t], 16 * NTURN * l)
                        elif not isinstance(i, int):
                            for t in range(HALF * q, HALF * (q + 1)):
                                act.wait_ge(gathered[t], 16 * (NTURN * l + i))
                        nc.scalar.copy(idx[:, q, :], src_sb[:, bass.ds((i * 2 + q) * HALF, HALF)]).then_inc(idx_ready, 1)
                    if l == 3:
                        for k in range(NK):
                            act.wait_ge(pre_ready, NK * i + k + 1)
                            after(act, block_summed, NB * 3 + NK * i + k - 1)
                            nc.scalar.activation(msg[:, k % 2], pre[:, k % 2].rearrange("p (t d) -> p t d", t=BT),
                                                 ACT.Silu).then_inc(msg_ready, 1)
                if l == 3:
                    act.wait_ge(flag_ready, 1)
                    n_left = act.value_load(left_flag[0:1, 0:1], min_val=0, max_val=EP)
                    with act.If(n_left > 0):
                        s = lf[3]
                        with act.Fori(0, NT) as t:
                            act.wait_ge(s["pre"], t + 1)
                            nc.scalar.activation(msg_left[:, :], pre_left[:, :], ACT.Silu).then_inc(s["msg"], 1)
                    break
                s = st[l + 1]
                for c, q, u in chunks(act):
                    act.wait_ge(s["z_mm"], c + 1)
                    after(act, s["turned"], c - 1)
                    if l == 0:
                        after(act, s["hT_ready"], c - 1)
                    if l == 1:
                        after(act, s["res_ready"], c - 1)
                    nc.scalar.activation(z[:, q], bank[q][:, :], ACT.Relu if l < 2 else ACT.Identity,
                                         bias=bcol[:, l:l + 1]).then_inc(s["z_ready"], 1)
                    if l < 2:
                        act.wait_ge(s["turned"], c + 1)
                        after(act, table_in[l + 1][q], 16 * u)
                        nc.scalar.copy(rows[:, q], pT(2 + q)).then_inc(s["rows_ready"], 1)
                    else:
                        ln_part(s, c, q)
                        after(act, s["res_ready"], c - 1)
                        nc.scalar.activation(hn[:, q], y[:, q], ACT.Relu).then_inc(s["hn_ready"], 1)
                        act.wait_ge(s["turned2"], c + 1)
                        after(act, s["row_mm"], c - 1)
                        after(act, s["hT_ready"], c - 1)
                        nc.scalar.copy(z2[:, q], bank[4 + q][:, :]).then_inc(s["z2_ready"], 1)
            s = st[4]
            for c, q, u in chunks(act):
                act.wait_ge(s["z_mm"], c + 1)
                after(act, s["row_mm"], c - 1)
                nc.scalar.activation(z[:, q], bank[q][:, :], ACT.Silu, bias=bcol[:, 3:4]).then_inc(s["z_ready"], 1)

        @block.tensor
        def _(pe):
            pe.wait_ge(const_built, 5)
            s = st[0]
            for c, q, u in chunks(pe):
                pe.wait_ge(s["hn_ready"], c + 1)
                after(pe, s["hT_ready"], c - 1)
                for j in range(JC):
                    m = nc.tensor.transpose(bank[2 + q][:, j * P:(j + 1) * P], hn[:, q, j, :], ident[:, :])
                m.then_inc(s["turned"], 1)
            pe.wait_ge(prep, 8)
            nc.tensor.matmul(bank[7][:, 0:1], ones[:, :], left_n[:, :], start=True, stop=True).then_inc(left_sum, 1)
            pe.wait_ge(consts_in, 16 * 11)
            pe.wait_ge(flag_ready, 1)

            def sum_block(l, i, k, rows_of):
                done = NB * l + NK * i + k
                pe.wait_ge(onehot_ready, done + 1)
                after(pe, added, done - NK + 1)
                for j in range(BT):
                    t = BT * k + j
                    if l < 3:
                        pe.wait_ge(gathered[t], 16 * (NTURN * l + i) + 16)
                    m = nc.tensor.matmul(bank[k][:, 0:W], rows_of(t), onehot[:, k, j, :], start=(j == 0), stop=(j == BT - 1))
                if l == 0:
                    for j in range(BT):
                        m = nc.tensor.matmul(bank[k][:, W:2 * W], ones[:, :], onehot[:, k, j, :], start=(j == 0), stop=(j == BT - 1))
                m.then_inc(block_summed, 1)

            def edge_products(i, k):
                done = NK * i + k
                if k % 2 == 0:
                    pe.wait_ge(ef_in[k // 2], 16 * i + 16)
                after(pe, pre_ready, done - 1)
                for j in range(BT):
                    t = (k % 2) * BT + j
                    m = nc.tensor.matmul(bank[4 + k % 2][:, j * D:(j + 1) * D], efT[:, k // 2, t * P:(t + 1) * P],
                                         mw[:, 1, :], start=True, stop=True)
                m.then_inc(edge_mm, 1)

            for l in range(4):
                for i in turns(pe):
                    if l < 3:
                        for k in range(NK):
                            sum_block(l, i, k, lambda t: gath[:, t, :])
                    else:
                        edge_products(i, 0)
                        for k in range(NK):
                            if k + 1 < NK:
                                edge_products(i, k + 1)
                            pe.wait_ge(msg_ready, NK * i + k + 1)
                            sum_block(3, i, k, lambda t: msg[:, (t // BT) % 2, t % BT, :])
                n_left = pe.value_load(left_flag[0:1, 0:1], min_val=0, max_val=EP)
                with pe.If(n_left > 0):
                    s = lf[l]
                    with pe.Fori(0, NT) as t:
                        if l == 3:
                            pe.wait_ge(s["ef_in"], 16 * t + 16)
                            nc.tensor.matmul(bank[7][:, 0:D], ef_left[:, :], mw[:, 1, :], start=True, stop=True).then_inc(s["edge_mm"], 1)
                            pe.wait_ge(s["msg"], t + 1)
                        else:
                            pe.wait_ge(s["gathered"], 16 * t + 16)
                        for k in range(NCH):
                            pe.wait_ge(s["onehot"], NCH * t + k + 1)
                            m = nc.tensor.matmul(bank[6][:, :], gath_left[:, :] if l < 3 else msg_left[:, :], hot_left[:, :],
                                                 start=True, stop=True)
                            if l == 0:
                                m = nc.tensor.matmul(bank[7][:, :], ones[:, :], hot_left[:, :], start=True, stop=True)
                            m.then_inc(s["summed"], 1)
                    pe.wait_ge(s["added"], NCH * NT + 1)
                if l == 3:
                    break
                s = st[l + 1]
                for c, q, u in chunks(pe):
                    pe.wait_ge(s["agg_ready"], c + 1)
                    after(pe, s["z_ready"], c - 1)
                    nc.tensor.matmul(bank[q][:, :], wl[:, l, :], agg[:, q, :], start=True, stop=False)
                    nc.tensor.matmul(bank[q][:, :], wr[:, l, :], hT[:, chunk_of(c)], start=False, stop=True).then_inc(s["z_mm"], 1)
                    pe.wait_ge(s["res_ready"] if l == 1 else s["z_ready"], c + 1)
                    after(pe, s["rows_ready"] if l < 2 else s["x1_ready"], c - 1)
                    of = z2 if l == 1 else z
                    for j in range(JC):
                        m = nc.tensor.transpose(bank[2 + q][:, j * P:(j + 1) * P], of[:, q, j * P:(j + 1) * P], ident[:, :])
                    m.then_inc(s["turned"], 1)
                    if l == 2:
                        pe.wait_ge(s["hn_ready"], c + 1)
                        after(pe, s["z2_ready"], c - 1)
                        for j in range(JC):
                            m = nc.tensor.transpose(bank[4 + q][:, j * P:(j + 1) * P], hn[:, q, j, :], ident[:, :])
                        m.then_inc(s["turned2"], 1)
                        pe.wait_ge(s["z2_ready"], c + 1)
                        after(pe, s["rows_ready"], c - 1)
                        for j in range(JC):
                            m = nc.tensor.matmul(bank[6 + q][:, j * P:(j + 1) * P], z2[:, q, j * P:(j + 1) * P], mw[:, 0, :],
                                                 start=True, stop=True)
                        m.then_inc(s["row_mm"], 1)
            s = st[4]
            pe.wait_ge(added, 4 * NB)
            for c, q, u in chunks(pe):
                after(pe, s["z_ready"], c - 1)
                nc.tensor.matmul(bank[q][:, :], uw[:, 0, :], hT[:, chunk_of(c)], start=True, stop=False)
                nc.tensor.matmul(bank[q][:, :], uw[:, 1, :], acc[:, 0, chunk_of(c)], start=False, stop=True).then_inc(s["z_mm"], 1)
                pe.wait_ge(s["z_ready"], c + 1)
                after(pe, s["rows_ready"], c - 1)
                for j in range(JC):
                    m = nc.tensor.matmul(bank[2 + q][:, j * P:(j + 1) * P], z[:, q, j * P:(j + 1) * P], uw2_sb[:, :],
                                         start=True, stop=True)
                m.then_inc(s["row_mm"], 1)

        @block.vector
        def _(dve):
            dve.wait_ge(const_built, 5)
            nc.vector.tensor_copy(iota_f[:, :], iota_i[:, :]).then_inc(prep, 1)

            def layernorm(s, c, q, of):
                for j in range(JC):
                    m = nc.vector.bn_stats(stats[:, q, j, :], of[:, q, j, :])
                m.then_inc(s["stats_ready"], 1)
                dve.wait_ge(s["stats_ready"], c + 1)
                after(dve, s["std_ready"], c - 1)
                apart(dve)
                for j in range(JC):
                    m = nc.vector.bn_aggr(meanvar[:, q, j, :], stats[:, q, j, :])
                m.then_inc(s["var_ready"], 1)
                dve.wait_ge(s["std_ready"], c + 1)
                nc.vector.reciprocal(rstd[:, q, :], std[:, q, :]).then_inc(s["rstd_ready"], 1)
                dve.wait_ge(s["rstd_ready"], c + 1)
                after(dve, s["hn_ready"], c - 1)
                for j in range(JC):
                    m = nc.vector.tensor_scalar(y[:, q, j, :], of[:, q, j, :], meanvar[:, q, j, 0:1], rstd[:, q, j:j + 1],
                                                ALU.subtract, ALU.mult)
                m.then_inc(s["y_ready"], 1)

            s = st[0]
            for c, q, u in chunks(dve):
                dve.wait_ge(s[f"x_in{q}"], 16 * u + 16)
                layernorm(s, c, q, xin)
                dve.wait_ge(s["turned"], c + 1)
                apart(dve)
                nc.vector.tensor_copy(hT[:, chunk_of(c)], bank[2 + q][:, :]).then_inc(s["hT_ready"], 1)

            dve.wait_ge(edges_in, 64)
            dst_b = dst_i[:, :].rearrange("p (b t) -> p b t", t=BT)
            first_b = first_i[:, :].rearrange("p (b o) -> p b o", o=1).to_broadcast([P, NB, BT])
            rel_f = rel[:, :, :].rearrange("p b t -> p (b t)")
            outside = agg[:, :, :].rearrange("p q n -> p (q n)")[:, 0:NT]
            real = z2[:, :, :].rearrange("p q n -> p (q n)")[:, 0:NT]
            nc.vector.tensor_tensor(rel[:, :, :], dst_b, first_b, ALU.subtract).then_inc(prep, 1)
            dve.wait_ge(prep, 2)
            nc.vector.tensor_scalar(outside, rel_f, 0.0, None, ALU.is_lt).then_inc(prep, 1)
            nc.vector.tensor_scalar(real, dst_i[:, :], float(N), None, ALU.is_lt)
            dve.wait_ge(prep, 3)
            nc.vector.scalar_tensor_tensor(out=outside, in0=rel_f, scalar=float(W), in1=outside, op0=ALU.is_ge, op1=ALU.add).then_inc(prep, 1)
            dve.wait_ge(prep, 4)
            nc.vector.tensor_tensor(outside, outside, real, ALU.mult).then_inc(prep, 1)
            dve.wait_ge(prep, 5)
            nc.vector.reduce_sum(left_n[:, :], outside, AX_X).then_inc(prep, 1)
            nc.vector.scalar_tensor_tensor(out=left[:, :], in0=dst_i[:, :], scalar=1.0, in1=outside, op0=ALU.add, op1=ALU.mult).then_inc(prep, 1)
            dve.wait_ge(prep, 7)
            nc.vector.tensor_scalar(left[:, :], left[:, :], -1.0, None, ALU.add).then_inc(prep, 1)
            dve.wait_ge(left_sum, 1)
            nc.vector.tensor_copy(left_flag[:, :], bank[7][:, 0:1]).then_inc(flag_ready, 1)
            dve.wait_ge(flag_ready, 1)
            iota_w = iota_f[:, 0:W].rearrange("p (o w) -> p o w", o=1).to_broadcast([P, BT, W])

            for l in range(4):
                R = 2 if l == 0 else 1
                nc.vector.memset(acc[:, 0:R, :], 0.0).then_inc(acc_zeroed, 1)
                dve.wait_ge(acc_zeroed, l + 1)

                def hot(i, k):
                    done = NB * l + NK * i + k
                    after(dve, block_summed, done - NK + 1)
                    b = rel[:, bass.ds(NK * i + k, 1), :].rearrange("p o t -> p t o").to_broadcast([P, BT, W])
                    nc.vector.tensor_tensor(onehot[:, k], iota_w, b, ALU.is_equal).then_inc(onehot_ready, 1)

                def add(i, k):
                    done = NB * l + NK * i + k
                    w0 = dve.value_load(first_row[0:1, bass.ds(NK * i + k, 1)], min_val=0, max_val=N - 1)
                    dve.wait_ge(block_summed, done + 1)
                    after(dve, added, done)
                    to = acc[:, 0:R, bass.ds(w0, W)]
                    nc.vector.tensor_tensor(to, to, bank[k][:, 0:R * W].rearrange("p (r w) -> p r w", r=R), ALU.add).then_inc(added, 1)

                def add_features(i, k):
                    done = NK * i + k
                    dve.wait_ge(edge_mm, done + 1)
                    for j in range(BT):
                        dve.wait_ge(gathered[BT * k + j], 16 * (NTURN * 3 + i) + 16)
                    after(dve, msg_ready, done - 1)
                    nc.vector.tensor_tensor(pre[:, k % 2], bank[4 + k % 2][:, :],
                                            gath[:, BT * k:BT * (k + 1), :].rearrange("p t d -> p (t d)"), ALU.add).then_inc(pre_ready, 1)

                for i in turns(dve):
                    for k in range(NK):
                        hot(i, k)
                        if l == 3:
                            add_features(i, k)
                            if k:
                                add(i, k - 1)
                    if l < 3:
                        for k in range(NK):
                            add(i, k)
                    else:
                        add(i, NK - 1)

                n_left = dve.value_load(left_flag[0:1, 0:1], min_val=0, max_val=EP)
                with dve.If(n_left > 0):
                    s = lf[l]
                    dve.wait_ge(added, NB * (l + 1))
                    nc.vector.memset(hot_left[:, :], 0.0).then_inc(s["added"], 1)
                    with dve.Fori(0, NT) as t:
                        if l == 3:
                            dve.wait_ge(s["edge_mm"], t + 1)
                            dve.wait_ge(s["gathered"], 16 * t + 16)
                            nc.vector.tensor_tensor(pre_left[:, :], bank[7][:, 0:D], gath_left[:, :], ALU.add).then_inc(s["pre"], 1)
                        for k in range(NCH):
                            dve.wait_ge(s["added"], NCH * t + k + 1)
                            nc.vector.tensor_scalar(hot_left[:, :], iota_f[:, :], float(CH * k), left[:, bass.ds(t, 1)],
                                                    ALU.add, ALU.is_equal).then_inc(s["onehot"], 1)
                            dve.wait_ge(s["summed"], NCH * t + k + 1)
                            to = acc[:, 0, k * CH:(k + 1) * CH]
                            m = nc.vector.tensor_tensor(to, to, bank[6][:, :], ALU.add)
                            if l == 0:
                                to = acc[:, 1, k * CH:(k + 1) * CH]
                                m = nc.vector.tensor_tensor(to, to, bank[7][:, :], ALU.add)
                            m.then_inc(s["added"], 1)
                    dve.wait_ge(s["added"], NCH * NT + 1)
                dve.wait_ge(added, NB * (l + 1))
                if l == 3:
                    break
                if l == 0:
                    nc.vector.tensor_scalar(acc[:, 1, :], acc[:, 1, :], 1.0, None, ALU.max).then_inc(degree_ready, 1)
                    dve.wait_ge(degree_ready, 1)
                    nc.vector.reciprocal(acc[:, 1, :], acc[:, 1, :]).then_inc(degree_ready, 1)
                    dve.wait_ge(degree_ready, 2)
                s = st[l + 1]
                for c, q, u in chunks(dve):
                    after(dve, s["z_mm"], c - 1)
                    nc.vector.tensor_tensor(agg[:, q, :], acc[:, 0, chunk_of(c)], acc[:, 1, chunk_of(c)], ALU.mult).then_inc(s["agg_ready"], 1)
                    if l == 0:
                        dve.wait_ge(s["z_ready"], c + 1)
                        apart(dve)
                        nc.vector.tensor_copy(hT[:, chunk_of(c)], z[:, q, :]).then_inc(s["hT_ready"], 1)
                    if l == 1:
                        dve.wait_ge(s["z_ready"], c + 1)
                        after(dve, s["turned"], c - 1)
                        nc.vector.tensor_tensor(z2[:, q, :], z[:, q, :], hT[:, chunk_of(c)], ALU.add).then_inc(s["res_ready"], 1)
                        dve.wait_ge(s["res_ready"], c + 1)
                        apart(dve)
                        nc.vector.tensor_copy(hT[:, chunk_of(c)], z2[:, q, :]).then_inc(s["hT_ready"], 1)
                    if l == 2:
                        dve.wait_ge(s["turned"], c + 1)
                        dve.wait_ge(s[f"x_in{q}"], 16 * u + 16)
                        nc.vector.tensor_tensor(x1[:, q], xin[:, q], pT(2 + q), ALU.add).then_inc(s["x1_ready"], 1)
                        dve.wait_ge(s["x1_ready"], c + 1)
                        layernorm(s, c, q, x1)
                        dve.wait_ge(s["hn_ready"], c + 1)
                        keep = acc[:, 1, chunk_of(c)].rearrange("p (j d) -> p j d", j=JC)
                        nc.vector.tensor_tensor(x1[:, q], x1[:, q], wide(ub2_row), ALU.add).then_inc(s["kept_part"], 1)
                        dve.wait_ge(s["z2_ready"], c + 1)
                        apart(dve)
                        nc.vector.tensor_copy(hT[:, chunk_of(c)], z2[:, q, :]).then_inc(s["hT_ready"], 1)
                        dve.wait_ge(s["kept_part"], c + 1)
                        dve.wait_ge(s["agg_ready"], c + 1)
                        nc.vector.tensor_tensor(keep, x1[:, q], hn[:, q], ALU.add).then_inc(s["res_ready"], 1)
                        dve.wait_ge(s["res_ready"], c + 1)
                        dve.wait_ge(s["row_mm"], c + 1)
                        after(dve, table_in[3][q], 16 * u)
                        nc.vector.tensor_tensor(rows[:, q], pT(6 + q), wide(mb1_row), ALU.add).then_inc(s["rows_ready"], 1)
            s = st[4]
            for c, q, u in chunks(dve):
                dve.wait_ge(s["row_mm"], c + 1)
                after(dve, out_written[q], 16 * u)
                keep = acc[:, 1, chunk_of(c)].rearrange("p (j d) -> p j d", j=JC)
                nc.vector.tensor_tensor(rows[:, q], pT(2 + q), keep, ALU.add).then_inc(s["rows_ready"], 1)


def kernel(**inputs):
    import numpy as np
    import concourse.bacc as bacc
    from concourse.bass_utils import run_bass_kernel_spmd

    a = {k: np.asarray(v) for k, v in inputs.items()}
    src = np.concatenate([a["src"], np.zeros(EP - E, a["src"].dtype)])
    dst = np.concatenate([a["dst"], np.full(EP - E, PAD_DST, a["dst"].dtype)])
    edge_T = np.zeros((D, EP), a["edge_attr_128"].dtype)
    edge_T[:, :E] = a["edge_attr_128"].T
    xp = np.zeros((NP, D), a["x"].dtype)
    xp[:N] = a["x"]
    arrays = {
        "x": xp,
        "src_t": np.ascontiguousarray(src.reshape(NT, P).T),
        "dst_t": np.ascontiguousarray(dst.reshape(NT, P).T),
        "dst_first": np.ascontiguousarray(dst[::BT * P].reshape(1, NB)),
        "edge_T": edge_T,
        "WlT": np.ascontiguousarray(np.stack([a[f"L0_gnn_W_l{k}"].T for k in (1, 2, 3)], axis=1)),
        "bl": np.stack([a[f"L0_gnn_b_l{k}"] for k in (1, 2, 3)]),
        "WrT": np.ascontiguousarray(np.stack([a[f"L0_gnn_W_r{k}"].T for k in (1, 2, 3)], axis=1)),
        "mw1": a["L1_gnn_mw1"], "mb1": a["L1_gnn_mb1"], "uw1": a["L1_gnn_uw1"], "ub1": a["L1_gnn_ub1"],
        "uw2": a["L1_gnn_uw2"], "ub2": a["L1_gnn_ub2"],
    }
    nc = bacc.Bacc("TRN2", target_bir_lowering=False, num_devices=1)
    args = [nc.dram_tensor(f"in_{n}", v.shape, mybir.dt.from_np(v.dtype), kind="ExternalInput").ap() for n, v in arrays.items()]
    out = nc.dram_tensor("out", (NP, D), F32, kind="ExternalOutput").ap()
    gnn_kernel(nc, *args, out)
    r = run_bass_kernel_spmd(nc, [{f"in_{n}": v for n, v in arrays.items()}], core_ids=[0])
    return r.results[0]["out"][:N]
```

```python
from contextlib import ExitStack

import concourse.bass as bass
from concourse import mybir

F32 = mybir.dt.float32
BF16 = mybir.dt.bfloat16
F16 = mybir.dt.float16
I32 = mybir.dt.int32
U32 = mybir.dt.uint32
ALU = mybir.AluOpType
ACT = mybir.ActivationFunctionType
AX_X = mybir.AxisListType.X

P = 128
N = 6250
D = 128
E = 106250
EPS = 1e-5

NTILE = -(-N // P)
NP = NTILE * P
JC = 4
CH = JC * P
NCH = -(-NTILE // JC)
JL = NTILE - (NCH - 1) * JC

BT = 3
W = 31
NA = NP + W
NK = 4
BODY = BT * NK
HALF = BODY // 2
NT = -(-E // (P * BT)) * BT
NB = NT // BT
FULL = NB // NK
LAST = NB - FULL * NK
EP = NT * P
PAD_DST = 8191
DT = 40
ROUND = 4 * NK
NR = DT * NK // ROUND
TR = (FULL + 1 - DT) // NR
CPAIR = 6
PAIRS = -(-DT * NK // CPAIR)
NSTAGE = 3
NC = PAIRS * CPAIR * BT
CW = NTILE * W
CS = CW + CW % 2
PIECE = [9] + [8] * 5
NPIECE = len(PIECE)
RING = 3
assert PAD_DST >= NP + W and 0 < LAST <= NK // 2 and sum(PIECE) == NTILE and CW <= 3 * 512 and ROUND * W <= 512
assert NR * ROUND == DT * NK and NR * TR == FULL + 1 - DT and NPIECE % RING == 0 and 2 * PAIRS <= FULL
assert TR * NK * 4 <= NTILE and BT * P <= 2048 and CPAIR % 2 == 0 and CPAIR % NSTAGE == 0

LAYER_TURNS = [FULL + 1, FULL + 1 - DT, FULL + 1 - DT, FULL + 1]
TURNS_BEFORE = [sum(LAYER_TURNS[:l]) for l in range(4)]
BLOCKS_BEFORE = [sum((n - 1) * NK + LAST for n in LAYER_TURNS[:l]) for l in range(5)]
HALVES_BEFORE = [sum(n * 2 for n in LAYER_TURNS[:l]) for l in range(4)]


def gathers_before(l, k):
    return TURNS_BEFORE[l] - (l if k >= LAST else 0)


def after(eng, sem, value):
    if not isinstance(value, int) or value > 0:
        eng.wait_ge(sem, value)


def turns(eng):
    yield 0, NK
    with eng.Fori(1, FULL) as i:
        yield i, NK
    yield FULL, LAST


def turns_counting(eng):
    def pair(j):
        for h in range(2):
            yield 2 * j + h, NK, [(CPAIR * j + n, n) for n in range(CPAIR // 2 * h, CPAIR // 2 * (h + 1))]
    yield from pair(0)
    with eng.Fori(1, PAIRS) as j:
        yield from pair(j)
    with eng.Fori(2 * PAIRS, FULL) as i:
        yield i, NK, []
    yield FULL, LAST, []


def rounds(eng):
    yield 0, [(g, NK) for g in range(TR)]
    with eng.Fori(1, NR - 1) as r:
        yield r, [(TR * r + g, NK) for g in range(TR)]
    yield NR - 1, [(TR * (NR - 1) + g, NK if g < TR - 1 else LAST) for g in range(TR)]


def layer_turns(eng, l):
    if l == 0:
        for i, nk, _ in turns_counting(eng):
            yield i, nk
    elif l == 3:
        yield from turns(eng)
    else:
        for r, group in rounds(eng):
            yield from group


def staggered(*stages):
    for at in range(NCH + max(lag for lag, _ in stages)):
        for lag, stage in stages:
            if 0 <= at - lag < NCH:
                c = at - lag
                stage(c, c % 2, JC if c < NCH - 1 else JL)


def gnn_kernel(nc, x, src_t, dst_t, dst_first, edge_T, WlT, bl, WrT, mw1, mb1, uw1, ub1, uw2, ub2, out):
    with ExitStack() as ctx:
        def sb(name, shape, dt=F32):
            return ctx.enter_context(nc.sbuf_tensor(name, shape, dt))

        def sem(name):
            return ctx.enter_context(nc.semaphore(name))

        bank = [ctx.enter_context(nc.psum_tensor(f"bank{b}", [P, 512], F32)) for b in range(8)]
        table = [nc.dram_tensor(f"table{l}", [NP, D], F32).ap() for l in range(4)]
        counts = nc.dram_tensor("counts", [PAIRS * CPAIR, P, CS], F16).ap()

        ident = sb("ident", [P, P])
        ones = sb("ones", [P, P])
        ones_h = sb("ones_h", [P, P], BF16)
        iota_f = sb("iota_f", [P, CH])
        iota_h = sb("iota_h", [P, CW], F16)
        wl = sb("wl", [P, 3, D])
        wr = sb("wr", [P, 3, D])
        mw = sb("mw", [P, 2, D])
        uw = sb("uw", [P, 2, D])
        uw2_sb = sb("uw2_sb", [P, D])
        bcol = sb("bcol", [P, 4])
        mb1_row = sb("mb1_row", [1, D])
        ub2_row = sb("ub2_row", [1, D])
        eps_col = sb("eps_col", [P, 1])

        src_sb = sb("src_sb", [P, (FULL + 1) * BODY], I32)
        first_row = sb("first_row", [1, NB], I32)
        rel = sb("rel", [P, NB, BT])
        left = sb("left", [P, NT])
        key = sb("key", [P, NC])
        low = sb("low", [P, NC])
        left_n = sb("left_n", [P, 1])
        left_flag = sb("left_flag", [P, 1], I32)

        hT = sb("hT", [P, NP])
        acc = sb("acc", [P, 2, NA])
        parts = sb("parts", [P, 3, NCH * JC, D], BF16)

        scratch = parts[:, :, :, :].rearrange("p a t d -> p (a t d)").bitcast(I32)
        iota_i = scratch[:, 0:CW]
        dst_i, first_i, src_high, src_low = (scratch[:, at:at + w] for at, w in
                                             [(2048, NT), (3072, NB), (4096, NC), (5120, NC)])

        idx = sb("idx", [P, 2, HALF], I32)
        gath = sb("gath", [P, BODY, D])
        onehot = sb("onehot", [P, NK, BT, W])
        onehot_h = onehot[:, :, :, :].rearrange("p k t w -> p (k t w)").bitcast(BF16).rearrange(
            "p (k t w h) -> p k t w h", k=NK, t=BT, h=2)
        HOT, LOWHOT, STAGE = 2 * BT * CS, 2 * BT * P, NSTAGE * CS
        region = sb("region", [P, HOT + LOWHOT + STAGE], BF16)
        pairhot = region[:, 0:HOT].rearrange("p (k j n) -> p k j n", k=2, j=BT)
        lowhot = region[:, HOT:HOT + LOWHOT].rearrange("p (k j n) -> p k j n", k=2, j=BT)
        stage = region[:, HOT + LOWHOT:].bitcast(F16).rearrange("p (k n) -> p k n", k=NSTAGE)
        ring = region[:, 0:RING * ROUND * PIECE[0] * W].bitcast(F16).rearrange("p (q b n) -> p q b n", q=RING, b=ROUND)
        EF, PRE = 2 * HALF * P, 2 * BT * D
        efT = region[:, 0:2 * EF].bitcast(F32).rearrange("p (q n) -> p q n", q=2)
        pre = region[:, 2 * EF:2 * EF + 2 * PRE].bitcast(F32).rearrange("p (q n) -> p q n", q=2)
        msg = region[:, 2 * EF + 2 * PRE:2 * EF + 4 * PRE].bitcast(F32).rearrange("p (q t d) -> p q t d", q=2, t=BT)
        dense_sum = sb("dense_sum", [P, ROUND * W])

        xin = sb("xin", [P, 2, JC, D])
        stats = sb("stats", [P, 2, JC, 6])
        meanvar = sb("meanvar", [P, 2, JC, 2])
        std = sb("std", [P, 2, JC])
        rstd = sb("rstd", [P, 2, JC])
        hn = sb("hn", [P, 2, JC, D])
        z = sb("z", [P, 2, CH])
        rows = sb("rows", [P, 2, JC, D])

        idx_left = sb("idx_left", [P, 1], I32)
        gath_left, ef_left, pre_left, msg_left = (xin[:, 0, j, :] for j in range(4))
        hot_left = z[:, 0, :]

        consts_in = sem("consts_in")
        passed = sem("passed")
        edges_in = sem("edges_in")
        const_built = sem("const_built")
        prep = sem("prep")
        PREP_LEFT = 15
        prep_act = sem("prep_act")
        left_sum = sem("left_sum")
        flag_ready = sem("flag_ready")
        idx_ready = sem("idx_ready")
        gathered = [sem(f"gathered{s}") for s in range(BODY)]
        onehot_ready = sem("onehot_ready")
        block_summed = sem("block_summed")
        added = sem("added")
        pairhot_ready = sem("pairhot_ready")
        block_counted = sem("block_counted")
        counts_ready = sem("counts_ready")
        counts_out = [sem(f"counts_out{k}") for k in range(NSTAGE)]
        counts_in = [sem(f"counts_in{q}") for q in range(RING)]
        piece_used = sem("piece_used")
        round_copied = sem("round_copied")
        dense_added = sem("dense_added")
        ef_in = [sem("ef_in0"), sem("ef_in1")]
        edge_mm = sem("edge_mm")
        pre_ready = sem("pre_ready")
        msg_ready = sem("msg_ready")
        acc_zeroed = sem("acc_zeroed")
        degree_ready = sem("degree_ready")
        out_written = [sem("out_written0"), sem("out_written1")]
        table_in = [[sem(f"table_in{l}_{q}") for q in range(2)] for l in range(4)]
        x_chunk_in = [sem(f"x_chunk_in{c}") for c in range(NCH)]
        x_in = [sem("x_in0"), sem("x_in1")]
        LN = ["stats_ready", "var_ready", "std_ready", "rstd_ready", "y_ready", "hn_ready", "turned", "hT_ready"]
        CONV = ["agg_ready", "z_mm", "z_ready", "turned", "rows_ready", "res_ready",
                "part0_ready", "part1_ready", "rest_ready", "parts_ready"]
        USED = [LN, CONV, CONV, LN + ["agg_ready", "z_mm", "z_ready", "x1_ready", "turned2", "row_mm", "rows_ready"],
                ["z_mm", "z_ready", "row_mm", "rows_ready"]]
        st = [{n: sem(f"n{k}_{n}") for n in names} for k, names in enumerate(USED)]
        LEFT = ["idx", "gathered", "onehot", "summed", "added"]
        lf = [{n: sem(f"left{l}_{n}") for n in LEFT + (["ef_in", "edge_mm", "pre", "msg"] if l == 3 else [])} for l in range(4)]

        def apart(eng):
            eng.sem_inc(passed, 1)

        def cols(c, n):
            return slice(c * CH, c * CH + n * P)

        def node_rows(t, c, n):
            return t[cols(c, n), :].rearrange("(j p) d -> p j d", p=P)

        def by_tile(b, n):
            return bank[b][:, 0:n * P].rearrange("p (j d) -> p j d", j=n)

        def kept(c, n):
            return acc[:, 1, cols(c, n)].rearrange("p (j d) -> p j d", j=n)

        def count_bank(k, b, w):
            return bank[(2 if k % 2 == 0 else 5) + b][:, 0:w]

        block = ctx.enter_context(nc.Block())

        @block.sync
        def _(sp):
            sp.dma_start(dst_i, dst_t).then_inc(edges_in, 16)
            sp.dma_start(first_i, dst_first.to_broadcast([P, NB])).then_inc(edges_in, 16)
            sp.dma_start(first_row[:, :], dst_first).then_inc(edges_in, 16)
            sp.dma_start(src_sb[:, :], src_t).then_inc(edges_in, 16)

            for c in range(NCH):
                n = JC if c < NCH - 1 else JL
                sp.dma_start(kept(c, n), node_rows(x, c, n)).then_inc(x_chunk_in[c], 16)
            for to, of in [(wl[:, :, :], WlT), (wr[:, :, :], WrT), (mw[:, :, :], mw1.rearrange("(t k) m -> k t m", t=2)),
                           (uw[:, :, :], uw1.rearrange("(t k) m -> k t m", t=2)), (uw2_sb[:, :], uw2),
                           (mb1_row[:, :], mb1.rearrange("(o d) -> o d", o=1)), (ub2_row[:, :], ub2.rearrange("(o d) -> o d", o=1))]:
                sp.dma_start(to, of).then_inc(consts_in, 16)
            for k in range(4):
                b = ub1 if k == 3 else bl[k]
                sp.dma_start(bcol[:, k:k + 1], b.rearrange("(d o) -> d o", o=1)).then_inc(consts_in, 16)

            def write_table(l, s, ready, of):
                def stage(c, q, n):
                    sp.wait_ge(s[ready], c + 1)
                    sp.dma_start(node_rows(table[l], c, n), of[:, q, 0:n]).then_inc(table_in[l][q], 16)
                return stage

            staggered((0, write_table(0, st[0], "hn_ready", hn)))

            for l in range(4):
                if l == 0:
                    for _, _, counted in turns_counting(sp):
                        for o, n in counted:
                            sp.wait_ge(counts_ready, o + 1)
                            sp.dma_start(counts[bass.ds(o, 1), :, 0:CW].rearrange("o p n -> (o p) n"),
                                         stage[:, n % NSTAGE, 0:CW]).then_inc(counts_out[n % NSTAGE], 16)
                    for k in range(NSTAGE):
                        sp.wait_ge(counts_out[k], 16 * PAIRS * CPAIR // NSTAGE)
                elif l < 3:
                    for r, _ in rounds(sp):
                        at = 0
                        for p, w in enumerate(PIECE):
                            after(sp, piece_used, NPIECE * (NR * (l - 1) + r) + p - RING + 1)
                            sp.dma_start(ring[:, p % RING, :, 0:w * W],
                                         counts[bass.ds(ROUND * r, ROUND), :, at * W:(at + w) * W].rearrange("b p n -> p b n")
                                         ).then_inc(counts_in[p % RING], 16)
                            at += w
                else:
                    for i, nk in turns(sp):
                        for q in range(-(-nk * BT // HALF)):
                            w = min(HALF, nk * BT - q * HALF) * P
                            after(sp, edge_mm, NK * (i - 1) + NK // 2 * (q + 1))
                            sp.dma_start(efT[:, q, 0:w], edge_T[:, bass.ds((i * 2 + q) * HALF * P, w)]).then_inc(ef_in[q], 16)
                sp.wait_ge(flag_ready, 1)
                n_left = sp.value_load(left_flag[0:1, 0:1], min_val=0, max_val=EP)
                with sp.If(n_left > 0):
                    s = lf[l]
                    with sp.Fori(0, NT) as t:
                        sp.wait_ge(s["added"], NCH * t + 1)
                        apart(sp)
                        sp.dma_start(idx_left[:, :], src_t[:, bass.ds(t, 1)],
                                     allow_slow_non_contiguous=True).then_inc(s["idx"], 16)
                        if l == 3:
                            sp.dma_start(ef_left, edge_T[:, bass.ds(t * P, P)]).then_inc(s["ef_in"], 16)
                    sp.wait_ge(s["added"], NCH * NT + 1)
                if l < 2:
                    staggered((0, write_table(l + 1, st[l + 1], "rows_ready", rows)))
                elif l == 2:
                    def load_x(c, q, n):
                        after(sp, st[3]["x1_ready"], c - 1)
                        sp.dma_start(xin[:, q, 0:n], node_rows(x, c, n)).then_inc(x_in[q], 16)

                    staggered((0, load_x), (5, write_table(3, st[3], "rows_ready", rows)))

            def write_out(c, q, n):
                sp.wait_ge(st[4]["rows_ready"], c + 1)
                sp.dma_start(node_rows(out, c, n), rows[:, q, 0:n]).then_inc(out_written[q], 16)

            staggered((0, write_out))
            sp.wait_ge(out_written[0], 16 * -(-NCH // 2))
            sp.wait_ge(out_written[1], 16 * (NCH // 2))

        @block.gpsimd
        def _(pool):
            nc.gpsimd.memset(ident[:, :], 0.0).then_inc(const_built, 1)
            nc.gpsimd.memset(ones[:, :], 1.0).then_inc(const_built, 1)
            nc.gpsimd.memset(ones_h[:, :], 1.0)
            nc.gpsimd.memset(eps_col[:, :], EPS).then_inc(const_built, 1)
            nc.gpsimd.iota(iota_i, pattern=[[1, CW]], base=0, channel_multiplier=0).then_inc(const_built, 1)
            pool.wait_ge(const_built, 4)
            nc.gpsimd.affine_select(out=ident[:, :], in_=ident[:, :], compare_op=ALU.not_equal, fill=1.0, base=0,
                                    pattern=[[-1, P]], channel_multiplier=1).then_inc(const_built, 1)

            for l in range(4):
                pool.wait_ge(table_in[l][0], 16 * -(-NCH // 2))
                pool.wait_ge(table_in[l][1], 16 * (NCH // 2))
                for m, nk in layer_turns(pool, l):
                    first = isinstance(m, int) and m == 0
                    for t in range(nk * BT):
                        k = t // BT
                        if t % HALF == 0:
                            pool.wait_ge(idx_ready, HALVES_BEFORE[l] + 2 * m + t // HALF + 1)
                        if t % BT == 0:
                            if l == 3:
                                after(pool, pre_ready, NK * (m - 1) + k + 1)
                            else:
                                after(pool, block_summed, BLOCKS_BEFORE[l] + (0 if first else NK * (m - 1) + k + 1))
                            apart(pool)
                        pool.indirect_dma_start(
                            out=gath[:, t, :], out_offset=None, in_=table[l],
                            in_offset=bass.IndirectOffsetOnAxis(ap=idx[:, t // HALF, t % HALF:t % HALF + 1].bitcast(U32), axis=0),
                        ).then_inc(gathered[t], 16)
                pool.wait_ge(flag_ready, 1)
                n_left = pool.value_load(left_flag[0:1, 0:1], min_val=0, max_val=EP)
                with pool.If(n_left > 0):
                    s = lf[l]
                    with pool.Fori(0, NT) as t:
                        pool.wait_ge(s["idx"], 16 * t + 16)
                        apart(pool)
                        pool.indirect_dma_start(
                            out=gath_left, out_offset=None, in_=table[l],
                            in_offset=bass.IndirectOffsetOnAxis(ap=idx_left[:, 0:1].bitcast(U32), axis=0),
                        ).then_inc(s["gathered"], 16)

        @block.scalar
        def _(act):
            act.wait_ge(const_built, 5)
            nc.scalar.copy(iota_h[:, :], iota_i).then_inc(prep_act, 1)

            def indices(l, m, q):
                for k in (2 * q, 2 * q + 1):
                    for t in range(BT * k, BT * (k + 1)):
                        after(act, gathered[t], 16 * (gathers_before(l, k) + m))
                if isinstance(m, int) and m == 0:
                    after(act, idx_ready, HALVES_BEFORE[l])
                turn = m + DT if l in (1, 2) else m
                nc.scalar.copy(idx[:, q, :], src_sb[:, bass.ds((turn * 2 + q) * HALF, HALF)]).then_inc(idx_ready, 1)

            def last_turn(l, m):
                return isinstance(m, int) and m == LAYER_TURNS[l] - 1

            def deviation(s):
                def stage(c, q, n):
                    act.wait_ge(s["var_ready"], c + 1)
                    nc.scalar.activation(std[:, q, 0:n], meanvar[:, q, 0:n, 1], ACT.Sqrt, bias=eps_col[:, 0:1]).then_inc(s["std_ready"], 1)
                return stage

            def positive(s):
                def stage(c, q, n):
                    act.wait_ge(s["y_ready"], c + 1)
                    nc.scalar.activation(hn[:, q, 0:n], hn[:, q, 0:n], ACT.Relu).then_inc(s["hn_ready"], 1)
                return stage

            def features(s, turned, b):
                def stage(c, q, n):
                    act.wait_ge(s[turned], c + 1)
                    nc.scalar.copy(hT[:, cols(c, n)], bank[b + q][:, 0:n * P]).then_inc(s["hT_ready"], 1)
                return stage

            act.wait_ge(edges_in, 64)
            for q in range(2):
                indices(0, 0, q)
            staggered((0, deviation(st[0])), (1, positive(st[0])), (2, features(st[0], "turned", 2)))
            act.wait_ge(consts_in, 16 * 11)

            def drain_round(l, r):
                act.wait_ge(piece_used, NPIECE * (NR * (l - 1) + r + 1))
                after(act, dense_added, ROUND * (NR * (l - 1) + r))
                nc.scalar.copy(dense_sum[:, :], bank[6][:, 0:ROUND * W]).then_inc(round_copied, 1)

            for l in range(4):
                if l == 0:
                    for i, nk, counted in turns_counting(act):
                        for o, n in counted:
                            act.wait_ge(block_counted, o + 1)
                            after(act, counts_out[n % NSTAGE], 16 * ((o - n) // CPAIR * (CPAIR // NSTAGE) + n // NSTAGE) if isinstance(o, int)
                                  else 16 * ((i // 2) * (CPAIR // NSTAGE) + n // NSTAGE))
                            for b in range(3):
                                w = min(512, CW - b * 512)
                                m = nc.scalar.copy(stage[:, n % NSTAGE, b * 512:b * 512 + w], count_bank(n, b, w))
                            m.then_inc(counts_ready, 1)
                            if n % (CPAIR // 2) == 1:
                                indices(0, i + 1, 0)
                        if not counted and not last_turn(0, i):
                            indices(0, i + 1, 0)
                        if not last_turn(0, i):
                            indices(0, i + 1, 1)
                elif l < 3:
                    for r, group in rounds(act):
                        for g, (m, nk) in enumerate(group):
                            if not last_turn(l, m):
                                indices(l, m + 1, 0)
                                indices(l, m + 1, 1)
                            if g == 0 and not (isinstance(r, int) and r == 0):
                                drain_round(l, r - 1)
                    drain_round(l, NR - 1)
                else:
                    for i, nk in turns(act):
                        for k in range(nk):
                            act.wait_ge(pre_ready, NK * i + k + 1)
                            after(act, block_summed, BLOCKS_BEFORE[3] + NK * i + k - 1)
                            nc.scalar.activation(msg[:, k % 2], pre[:, k % 2].rearrange("p (t d) -> p t d", t=BT),
                                                 ACT.Silu).then_inc(msg_ready, 1)
                            if k % 2 == 1:
                                indices(3, i + 1, k // 2)
                if l < 3:
                    for q in range(2):
                        indices(l + 1, 0, q)
                if l == 3:
                    act.wait_ge(flag_ready, 1)
                    n_left = act.value_load(left_flag[0:1, 0:1], min_val=0, max_val=EP)
                    with act.If(n_left > 0):
                        s = lf[3]
                        with act.Fori(0, NT) as t:
                            act.wait_ge(s["pre"], t + 1)
                            nc.scalar.activation(msg_left, pre_left, ACT.Silu).then_inc(s["msg"], 1)
                elif l < 2:
                    s = st[l + 1]

                    def convolved(c, q, n):
                        act.wait_ge(s["z_mm"], c + 1)
                        to = hT[:, cols(c, n)] if l == 0 else z[:, q, 0:n * P]
                        if l == 1:
                            after(act, s["res_ready"], c - 1)
                        nc.scalar.activation(to, bank[q][:, 0:n * P], ACT.Relu, bias=bcol[:, l:l + 1]).then_inc(s["z_ready"], 1)

                    def by_rows(c, q, n):
                        act.wait_ge(s["turned"], c + 1)
                        after(act, table_in[l + 1][q], 16 * (c // 2))
                        after(act, s["rest_ready"], c - 1)
                        nc.scalar.copy(rows[:, q, 0:n], by_tile(2 + q, n)).then_inc(s["rows_ready"], 1)
                        nc.scalar.copy(parts[:, 0, c * JC:c * JC + n, :], by_tile(2 + q, n)).then_inc(s["part0_ready"], 1)

                    def second_part(c, q, n):
                        act.wait_ge(s["rest_ready"], c + 1)
                        nc.scalar.copy(parts[:, 1, c * JC:c * JC + n, :], hn[:, q, 0:n]).then_inc(s["part1_ready"], 1)

                    staggered((0, convolved), (1, by_rows), (2, second_part))
                else:
                    s = st[3]

                    def convolved(c, q, n):
                        act.wait_ge(s["z_mm"], c + 1)
                        after(act, s["turned"], c - 1)
                        nc.scalar.activation(z[:, q, 0:n * P], bank[q][:, 0:n * P], ACT.Identity, bias=bcol[:, 2:3]).then_inc(s["z_ready"], 1)

                    def by_rows(c, q, n):
                        act.wait_ge(s["row_mm"], c + 1)
                        after(act, table_in[3][q], 16 * (c // 2))
                        nc.scalar.copy(rows[:, q, 0:n], by_tile(6 + q, n)).then_inc(s["rows_ready"], 1)

                    staggered((0, convolved), (1, deviation(s)), (2, positive(s)), (3, features(s, "turned2", 4)), (4, by_rows))
            s = st[4]

            def updated(c, q, n):
                act.wait_ge(s["z_mm"], c + 1)
                after(act, s["row_mm"], c - 1)
                nc.scalar.activation(z[:, q, 0:n * P], bank[q][:, 0:n * P], ACT.Silu, bias=bcol[:, 3:4]).then_inc(s["z_ready"], 1)

            staggered((0, updated))

        @block.tensor
        def _(pe):
            pe.wait_ge(const_built, 5)

            def turn_rows(s, turned, b):
                def stage(c, q, n):
                    pe.wait_ge(s["hn_ready"], c + 1)
                    after(pe, s["hT_ready"], c - 1)
                    for j in range(n):
                        m = nc.tensor.transpose(bank[b + q][:, j * P:(j + 1) * P], hn[:, q, j, :], ident[:, :])
                    m.then_inc(s[turned], 1)
                return stage

            staggered((0, turn_rows(st[0], "turned", 2)))
            pe.wait_ge(st[0]["hT_ready"], NCH)
            pe.wait_ge(prep, PREP_LEFT)
            nc.tensor.matmul(bank[7][:, 0:1], ones[:, :], left_n[:, :], start=True, stop=True).then_inc(left_sum, 1)
            pe.wait_ge(consts_in, 16 * 11)
            pe.wait_ge(flag_ready, 1)

            def sum_block(l, m, k, rows_of):
                done = BLOCKS_BEFORE[l] + NK * m + k
                pe.wait_ge(onehot_ready, done + 1)
                after(pe, added, done - 1)
                for j in range(BT):
                    t = BT * k + j
                    if l < 3:
                        pe.wait_ge(gathered[t], 16 * (gathers_before(l, k) + m) + 16)
                    mm = nc.tensor.matmul(bank[k % 2][:, 0:W], rows_of(t), onehot[:, k, j, :], start=(j == 0), stop=(j == BT - 1))
                if l == 0:
                    for j in range(BT):
                        mm = nc.tensor.matmul(bank[k % 2][:, W:2 * W], ones_h[:, :], onehot_h[:, k, j, :, 1], start=(j == 0), stop=(j == BT - 1))
                mm.then_inc(block_summed, 1)

            def count_block(o, n):
                pe.wait_ge(pairhot_ready, o + 1)
                after(pe, counts_ready, o - 1)
                for j in range(BT):
                    for b in range(3):
                        w = min(512, CW - b * 512)
                        mm = nc.tensor.matmul(count_bank(n, b, w), lowhot[:, n % 2, j, :], pairhot[:, n % 2, j, b * 512:b * 512 + w],
                                              start=(j == 0), stop=(j == BT - 1))
                mm.then_inc(block_counted, 1)

            def edge_products(i, k):
                done = NK * i + k
                if k % 2 == 0:
                    pe.wait_ge(ef_in[k // 2], 16 * i + 16)
                after(pe, pre_ready, done - 1)
                for j in range(BT):
                    t = (k % 2) * BT + j
                    mm = nc.tensor.matmul(bank[4 + k % 2][:, j * D:(j + 1) * D], efT[:, k // 2, t * P:(t + 1) * P],
                                          mw[:, 1, :], start=True, stop=True)
                mm.then_inc(edge_mm, 1)

            for l in range(4):
                if l == 0:
                    for i, nk, counted in turns_counting(pe):
                        for k in range(nk):
                            sum_block(0, i, k, lambda t: gath[:, t, :])
                            if k < len(counted):
                                count_block(*counted[k])
                elif l < 3:
                    for r, group in rounds(pe):
                        blocks = [(m, k) for m, nk in group for k in range(nk)]
                        ordinal = NR * (l - 1) + r
                        hi = 0
                        for p, w in enumerate(PIECE):
                            for h in range(w):
                                if hi % 4 == 0 and hi // 4 < len(blocks):
                                    m, k = blocks[hi // 4]
                                    sum_block(l, m, k, lambda t: gath[:, t, :])
                                if h == 0:
                                    pe.wait_ge(counts_in[p % RING], 16 * (NPIECE // RING * ordinal + p // RING + 1))
                                if hi == 0:
                                    after(pe, round_copied, ordinal)
                                for a in range(3):
                                    mm = nc.tensor.matmul(bank[6][:, 0:ROUND * W].rearrange("p (b n) -> p b n", b=ROUND), parts[:, a, hi, :],
                                                          ring[:, p % RING, :, h * W:(h + 1) * W],
                                                          start=(hi == 0 and a == 0), stop=(hi == NTILE - 1 and a == 2))
                                hi += 1
                            mm.then_inc(piece_used, 1)
                else:
                    for i, nk in turns(pe):
                        edge_products(i, 0)
                        for k in range(nk):
                            if k + 1 < nk:
                                edge_products(i, k + 1)
                            pe.wait_ge(msg_ready, NK * i + k + 1)
                            sum_block(3, i, k, lambda t: msg[:, (t // BT) % 2, t % BT, :])
                n_left = pe.value_load(left_flag[0:1, 0:1], min_val=0, max_val=EP)
                with pe.If(n_left > 0):
                    s = lf[l]
                    with pe.Fori(0, NT) as t:
                        if l == 3:
                            pe.wait_ge(s["ef_in"], 16 * t + 16)
                            nc.tensor.matmul(bank[5][:, 0:D], ef_left, mw[:, 1, :], start=True, stop=True).then_inc(s["edge_mm"], 1)
                            pe.wait_ge(s["msg"], t + 1)
                        else:
                            pe.wait_ge(s["gathered"], 16 * t + 16)
                        for c in range(NCH):
                            w = min(CH, NP - c * CH)
                            pe.wait_ge(s["onehot"], NCH * t + c + 1)
                            mm = nc.tensor.matmul(bank[4][:, 0:w], gath_left if l < 3 else msg_left, hot_left[:, 0:w],
                                                  start=True, stop=True)
                            if l == 0:
                                mm = nc.tensor.matmul(bank[5][:, 0:w], ones[:, :], hot_left[:, 0:w], start=True, stop=True)
                            mm.then_inc(s["summed"], 1)
                    pe.wait_ge(s["added"], NCH * NT + 1)
                if l == 3:
                    break
                s = st[l + 1]

                def convolve(c, q, n):
                    pe.wait_ge(s["agg_ready"], c + 1)
                    after(pe, s["z_ready"], c - 1)
                    nc.tensor.matmul(bank[q][:, 0:n * P], wl[:, l, :], acc[:, 0, cols(c, n)], start=True, stop=False)
                    nc.tensor.matmul(bank[q][:, 0:n * P], wr[:, l, :], hT[:, cols(c, n)], start=False, stop=True).then_inc(s["z_mm"], 1)

                def turn_features(c, q, n):
                    pe.wait_ge(s["res_ready"] if l == 1 else s["z_ready"], c + 1)
                    after(pe, s["part0_ready"] if l < 2 else s["x1_ready"], c - 1)
                    for j in range(n):
                        of = z[:, q, j * P:(j + 1) * P] if l == 2 else hT[:, c * CH + j * P:c * CH + (j + 1) * P]
                        mm = nc.tensor.transpose(bank[2 + q][:, j * P:(j + 1) * P], of, ident[:, :])
                    mm.then_inc(s["turned"], 1)

                def message_rows(c, q, n):
                    pe.wait_ge(s["hT_ready"], c + 1)
                    after(pe, s["rows_ready"], c - 1)
                    for j in range(n):
                        to = bank[6 + q][:, j * P:(j + 1) * P]
                        nc.tensor.matmul(to, hT[:, c * CH + j * P:c * CH + (j + 1) * P], mw[:, 0, :], start=True, stop=False)
                        mm = nc.tensor.matmul(to, ones[0:1, :], mb1_row[:, :], start=False, stop=True)
                    mm.then_inc(s["row_mm"], 1)

                if l < 2:
                    staggered((0, convolve), (1, turn_features))
                else:
                    staggered((0, convolve), (1, turn_features), (2, turn_rows(s, "turned2", 4)), (3, message_rows))
                    pe.wait_ge(s["hT_ready"], NCH)
            s = st[4]
            pe.wait_ge(added, BLOCKS_BEFORE[4])

            def update(c, q, n):
                after(pe, s["z_ready"], c - 1)
                nc.tensor.matmul(bank[q][:, 0:n * P], uw[:, 0, :], hT[:, cols(c, n)], start=True, stop=False)
                nc.tensor.matmul(bank[q][:, 0:n * P], uw[:, 1, :], acc[:, 0, cols(c, n)], start=False, stop=True).then_inc(s["z_mm"], 1)

            def update_rows(c, q, n):
                pe.wait_ge(s["z_ready"], c + 1)
                after(pe, s["rows_ready"], c - 1)
                for j in range(n):
                    to = bank[2 + q][:, j * P:(j + 1) * P]
                    nc.tensor.matmul(to, z[:, q, j * P:(j + 1) * P], uw2_sb[:, :], start=True, stop=False)
                    nc.tensor.matmul(to, hT[:, c * CH + j * P:c * CH + (j + 1) * P], ident[:, :], start=False, stop=False)
                    mm = nc.tensor.matmul(to, ones[0:1, :], ub2_row[:, :], start=False, stop=True)
                mm.then_inc(s["row_mm"], 1)

            staggered((0, update), (1, update_rows))

        @block.vector
        def _(dve):
            dve.wait_ge(const_built, 5)
            nc.vector.tensor_copy(iota_f[:, :], iota_i[:, 0:CH])

            def statistics(s, before):
                def stage(c, q, n):
                    before(c, q, n)
                    of = kept(c, n)
                    for j in range(n):
                        m = nc.vector.bn_stats(stats[:, q, j, :], of[:, j, :])
                    m.then_inc(s["stats_ready"], 1)
                    dve.wait_ge(s["stats_ready"], c + 1)
                    after(dve, s["std_ready"], c - 1)
                    for j in range(n):
                        m = nc.vector.bn_aggr(meanvar[:, q, j, :], stats[:, q, j, :])
                    m.then_inc(s["var_ready"], 1)
                return stage

            def normalise(s, written):
                def stage(c, q, n):
                    of = kept(c, n)
                    dve.wait_ge(s["std_ready"], c + 1)
                    nc.vector.reciprocal(rstd[:, q, 0:n], std[:, q, 0:n]).then_inc(s["rstd_ready"], 1)
                    dve.wait_ge(s["rstd_ready"], c + 1)
                    after(dve, s["turned2"] if written is None else s["turned"], c - 1)
                    if written is not None:
                        after(dve, written[q], 16 * (c // 2))
                    for j in range(n):
                        m = nc.vector.tensor_scalar(hn[:, q, j, :], of[:, j, :], meanvar[:, q, j, 0:1], rstd[:, q, j:j + 1],
                                                    ALU.subtract, ALU.mult)
                    m.then_inc(s["y_ready"], 1)
                return stage

            def x_loaded(c, q, n):
                dve.wait_ge(x_chunk_in[c], 16)

            staggered((0, statistics(st[0], x_loaded)), (1, normalise(st[0], table_in[0])))

            dve.wait_ge(edges_in, 64)
            steps = [0]

            def step(ins):
                steps[0] += 1
                ins.then_inc(prep, 1)
                dve.wait_ge(prep, steps[0])

            dst_b = dst_i.rearrange("p (b t) -> p b t", t=BT)
            first_b = first_i.rearrange("p (b o) -> p b o", o=1).to_broadcast([P, NB, BT])
            rel_f = rel[:, :, :].rearrange("p b t -> p (b t)")
            outside = xin[:, :, :, :].rearrange("p q j d -> p (q j d)")[:, 0:NT]
            real = z[:, :, :].rearrange("p q n -> p (q n)")[:, 0:NT]
            step(nc.vector.tensor_tensor(rel[:, :, :], dst_b, first_b, ALU.subtract))
            step(nc.vector.tensor_scalar(outside, rel_f, 0.0, None, ALU.is_lt))
            step(nc.vector.tensor_scalar(real, dst_i, float(N), None, ALU.is_lt))
            step(nc.vector.scalar_tensor_tensor(out=outside, in0=rel_f, scalar=float(W), in1=outside, op0=ALU.is_ge, op1=ALU.add))
            step(nc.vector.tensor_scalar(src_high, src_sb[:, 0:NC], 7, None, ALU.arith_shift_right))
            step(nc.vector.tensor_scalar(src_low, src_sb[:, 0:NC], P - 1, None, ALU.bitwise_and))
            step(nc.vector.tensor_copy(low[:, :], src_low))
            step(nc.vector.scalar_tensor_tensor(out=key[:, :], in0=src_high, scalar=float(W), in1=rel_f[:, 0:NC], op0=ALU.mult, op1=ALU.add))
            step(nc.vector.tensor_scalar(left[:, 0:NC], outside[:, 0:NC], -1.0, 1.0, ALU.mult, ALU.add))
            step(nc.vector.scalar_tensor_tensor(out=key[:, :], in0=key[:, :], scalar=1.0, in1=left[:, 0:NC], op0=ALU.add, op1=ALU.mult))
            step(nc.vector.tensor_scalar(key[:, :], key[:, :], -1.0, None, ALU.add))
            step(nc.vector.tensor_tensor(outside, outside, real, ALU.mult))
            step(nc.vector.scalar_tensor_tensor(out=left[:, :], in0=dst_i, scalar=1.0, in1=outside, op0=ALU.add, op1=ALU.mult))
            step(nc.vector.tensor_scalar(left[:, :], left[:, :], -1.0, None, ALU.add))
            step(nc.vector.reduce_sum(left_n[:, :], outside, AX_X))
            assert steps[0] == PREP_LEFT
            dve.wait_ge(left_sum, 1)
            nc.vector.tensor_copy(left_flag[:, :], bank[7][:, 0:1]).then_inc(flag_ready, 1)
            dve.wait_ge(flag_ready, 1)
            dve.wait_ge(prep_act, 1)
            iota_w = iota_f[:, 0:W].rearrange("p (o w) -> p o w", o=1).to_broadcast([P, BT, W])

            for l in range(4):
                R = 2 if l == 0 else 1
                nc.vector.memset(acc[:, 0:R, :], 0.0).then_inc(acc_zeroed, 1)
                dve.wait_ge(acc_zeroed, l + 1)

                def hot(m, k, turn):
                    first = isinstance(m, int) and m == 0
                    after(dve, block_summed, BLOCKS_BEFORE[l] + (0 if first else NK * (m - 1) + k + 1))
                    b = rel[:, bass.ds(NK * turn + k, 1), :].rearrange("p o t -> p t o").to_broadcast([P, BT, W])
                    nc.vector.tensor_tensor(onehot[:, k], iota_w, b, ALU.is_equal).then_inc(onehot_ready, 1)

                def add(m, k, turn):
                    done = BLOCKS_BEFORE[l] + NK * m + k
                    w0 = dve.value_load(first_row[0:1, bass.ds(NK * turn + k, 1)], min_val=0, max_val=N - 1)
                    dve.wait_ge(block_summed, done + 1)
                    after(dve, added, done)
                    to = acc[:, 0:R, bass.ds(w0, W)]
                    nc.vector.tensor_tensor(to, to, bank[k % 2][:, 0:R * W].rearrange("p (r w) -> p r w", r=R), ALU.add).then_inc(added, 1)

                def add_dense(r, b, before):
                    ordinal = ROUND * (NR * (l - 1) + r) + b
                    w0 = dve.value_load(first_row[0:1, bass.ds(ROUND * r + b, 1)], min_val=0, max_val=N - 1)
                    if b == 0:
                        dve.wait_ge(round_copied, NR * (l - 1) + r + 1)
                    if b % (ROUND // 4) == 0:
                        dve.wait_ge(added, before)
                    after(dve, dense_added, ordinal)
                    to = acc[:, 0, bass.ds(w0, W)]
                    nc.vector.tensor_tensor(to, to, dense_sum[:, b * W:(b + 1) * W], ALU.add).then_inc(dense_added, 1)

                def pair_hot(o, n):
                    after(dve, block_counted, o - 1)
                    for j in range(BT):
                        t = bass.ds(BT * o + j, 1)
                        nc.vector.tensor_scalar(lowhot[:, n % 2, j, :], iota_h[:, 0:P], low[:, t], None, ALU.is_equal)
                        m = nc.vector.tensor_scalar(pairhot[:, n % 2, j, 0:CW], iota_h[:, :], key[:, t], None, ALU.is_equal)
                    m.then_inc(pairhot_ready, 1)

                def add_features(i, k):
                    done = NK * i + k
                    dve.wait_ge(edge_mm, done + 1)
                    for j in range(BT):
                        dve.wait_ge(gathered[BT * k + j], 16 * (gathers_before(3, k) + i) + 16)
                    after(dve, msg_ready, done - 1)
                    nc.vector.tensor_tensor(pre[:, k % 2], bank[4 + k % 2][:, 0:BT * D],
                                            gath[:, BT * k:BT * (k + 1), :].rearrange("p t d -> p (t d)"), ALU.add).then_inc(pre_ready, 1)

                if l == 0:
                    for i, nk, counted in turns_counting(dve):
                        for k in range(nk):
                            hot(i, k, i)
                            if k < len(counted):
                                pair_hot(*counted[k])
                            if k:
                                add(i, k - 1, i)
                        add(i, nk - 1, i)
                elif l == 3:
                    for i, nk in turns(dve):
                        for k in range(nk):
                            hot(i, k, i)
                            add_features(i, k)
                            if k:
                                add(i, k - 1, i)
                        add(i, nk - 1, i)
                else:
                    for r, group in rounds(dve):
                        blocks = [(m, k) for m, nk in group for k in range(nk)]
                        for n, (m, k) in enumerate(blocks):
                            hot(m, k, m + DT)
                            if n:
                                add(*blocks[n - 1], blocks[n - 1][0] + DT)
                            if n in (1, 2, 3, 4) and not (isinstance(r, int) and r == 0):
                                before = BLOCKS_BEFORE[l] + NK * TR * r + n
                                for b in range(ROUND // 4 * (n - 1), ROUND // 4 * n):
                                    add_dense(r - 1, b, before)
                                dve.wait_ge(dense_added, ROUND * (NR * (l - 1) + r - 1) + ROUND // 4 * n)
                        add(*blocks[-1], blocks[-1][0] + DT)
                    for b in range(ROUND):
                        add_dense(NR - 1, b, BLOCKS_BEFORE[l + 1])
                    dve.wait_ge(dense_added, ROUND * NR * l)

                n_left = dve.value_load(left_flag[0:1, 0:1], min_val=0, max_val=EP)
                dve.wait_ge(added, BLOCKS_BEFORE[l + 1])
                with dve.If(n_left > 0):
                    s = lf[l]
                    nc.vector.memset(hot_left, 0.0).then_inc(s["added"], 1)
                    with dve.Fori(0, NT) as t:
                        if l == 3:
                            dve.wait_ge(s["edge_mm"], t + 1)
                            dve.wait_ge(s["gathered"], 16 * t + 16)
                            nc.vector.tensor_tensor(pre_left, bank[5][:, 0:D], gath_left, ALU.add).then_inc(s["pre"], 1)
                        for c in range(NCH):
                            w = min(CH, NP - c * CH)
                            dve.wait_ge(s["added"], NCH * t + c + 1)
                            nc.vector.tensor_scalar(hot_left, iota_f[:, :], float(CH * c), left[:, bass.ds(t, 1)],
                                                    ALU.add, ALU.is_equal).then_inc(s["onehot"], 1)
                            dve.wait_ge(s["summed"], NCH * t + c + 1)
                            to = acc[:, 0, c * CH:c * CH + w]
                            m = nc.vector.tensor_tensor(to, to, bank[4][:, 0:w], ALU.add)
                            if l == 0:
                                to = acc[:, 1, c * CH:c * CH + w]
                                m = nc.vector.tensor_tensor(to, to, bank[5][:, 0:w], ALU.add)
                            m.then_inc(s["added"], 1)
                    dve.wait_ge(s["added"], NCH * NT + 1)
                if l == 3:
                    break
                if l == 0:
                    nc.vector.tensor_scalar(acc[:, 1, :], acc[:, 1, :], 1.0, None, ALU.max).then_inc(degree_ready, 1)
                    dve.wait_ge(degree_ready, 1)
                    nc.vector.reciprocal(acc[:, 1, :], acc[:, 1, :]).then_inc(degree_ready, 1)
                    dve.wait_ge(degree_ready, 2)
                s = st[l + 1]

                def average(c, q, n):
                    to = acc[:, 0, cols(c, n)]
                    nc.vector.tensor_tensor(to, to, acc[:, 1, cols(c, n)], ALU.mult).then_inc(s["agg_ready"], 1)

                def add_input(c, q, n):
                    dve.wait_ge(s["z_ready"], c + 1)
                    to = hT[:, cols(c, n)]
                    nc.vector.tensor_tensor(to, z[:, q, 0:n * P], to, ALU.add).then_inc(s["res_ready"], 1)

                def first_rest(c, q, n):
                    dve.wait_ge(s["part0_ready"], c + 1)
                    after(dve, s["parts_ready"], c - 1)
                    after(dve, s["part1_ready"], c - 1)
                    nc.vector.tensor_tensor(hn[:, q, 0:n], rows[:, q, 0:n], parts[:, 0, c * JC:c * JC + n, :], ALU.subtract).then_inc(s["rest_ready"], 1)

                def third_part(c, q, n):
                    dve.wait_ge(s["part1_ready"], c + 1)
                    nc.vector.tensor_tensor(parts[:, 2, c * JC:c * JC + n, :], hn[:, q, 0:n], parts[:, 1, c * JC:c * JC + n, :],
                                            ALU.subtract).then_inc(s["parts_ready"], 1)

                def residual(c, q, n):
                    dve.wait_ge(s["turned"], c + 1)
                    dve.wait_ge(x_in[q], 16 * (c // 2) + 16)
                    nc.vector.tensor_tensor(kept(c, n), xin[:, q, 0:n], by_tile(2 + q, n), ALU.add).then_inc(s["x1_ready"], 1)
                    dve.wait_ge(s["x1_ready"], c + 1)

                if l == 0:
                    staggered((0, average), (2, first_rest), (3, third_part))
                elif l == 1:
                    staggered((0, average), (1, add_input), (3, first_rest), (4, third_part))
                else:
                    staggered((0, average), (1, statistics(s, residual)), (2, normalise(s, None)))
            s = st[4]

            def result(c, q, n):
                dve.wait_ge(s["row_mm"], c + 1)
                after(dve, out_written[q], 16 * (c // 2))
                nc.vector.tensor_tensor(rows[:, q, 0:n], by_tile(2 + q, n), kept(c, n), ALU.add).then_inc(s["rows_ready"], 1)

            staggered((0, result))


def kernel(**inputs):
    import numpy as np
    import concourse.bacc as bacc
    from concourse.bass_utils import run_bass_kernel_spmd

    a = {k: np.asarray(v) for k, v in inputs.items()}
    src = np.concatenate([a["src"], np.zeros((FULL + 1) * BODY * P - E, a["src"].dtype)])
    dst = np.concatenate([a["dst"], np.full(EP - E, PAD_DST, a["dst"].dtype)])
    edge_T = np.zeros((D, EP), a["edge_attr_128"].dtype)
    edge_T[:, :E] = a["edge_attr_128"].T
    xp = np.zeros((NP, D), a["x"].dtype)
    xp[:N] = a["x"]
    arrays = {
        "x": xp,
        "src_t": np.ascontiguousarray(src.reshape(-1, P).T),
        "dst_t": np.ascontiguousarray(dst.reshape(NT, P).T),
        "dst_first": np.ascontiguousarray(dst[::BT * P].reshape(1, NB)),
        "edge_T": edge_T,
        "WlT": np.ascontiguousarray(np.stack([a[f"L0_gnn_W_l{k}"].T for k in (1, 2, 3)], axis=1)),
        "bl": np.stack([a[f"L0_gnn_b_l{k}"] for k in (1, 2, 3)]),
        "WrT": np.ascontiguousarray(np.stack([a[f"L0_gnn_W_r{k}"].T for k in (1, 2, 3)], axis=1)),
        "mw1": a["L1_gnn_mw1"], "mb1": a["L1_gnn_mb1"], "uw1": a["L1_gnn_uw1"], "ub1": a["L1_gnn_ub1"],
        "uw2": a["L1_gnn_uw2"], "ub2": a["L1_gnn_ub2"],
    }
    nc = bacc.Bacc("TRN2", target_bir_lowering=False, num_devices=1)
    args = [nc.dram_tensor(f"in_{n}", v.shape, mybir.dt.from_np(v.dtype), kind="ExternalInput").ap() for n, v in arrays.items()]
    out = nc.dram_tensor("out", (NP, D), F32, kind="ExternalOutput").ap()
    gnn_kernel(nc, *args, out)
    r = run_bass_kernel_spmd(nc, [{f"in_{n}": v for n, v in arrays.items()}], core_ids=[0])
    return r.results[0]["out"][:N]
```

```python
from contextlib import ExitStack

import concourse.bass as bass
from concourse import mybir

F32 = mybir.dt.float32
BF16 = mybir.dt.bfloat16
F16 = mybir.dt.float16
I32 = mybir.dt.int32
U32 = mybir.dt.uint32
ALU = mybir.AluOpType
ACT = mybir.ActivationFunctionType
AX_X = mybir.AxisListType.X

P = 128
N = 6250
D = 128
E = 106250
EPS = 1e-5

NTILE = -(-N // P)
NP = NTILE * P
JC = 4
CH = JC * P
NCH = -(-NTILE // JC)
JL = NTILE - (NCH - 1) * JC

BT = 3
W = 31
NA = NP + W
NK = 4
BODY = BT * NK
HALF = BODY // 2
NT = -(-E // (P * BT)) * BT
NB = NT // BT
FULL = NB // NK
LAST = NB - FULL * NK
EP = NT * P
PAD_DST = 8191
DT = 40
ROUND = 4 * NK
NR = DT * NK // ROUND
TR = (FULL + 1 - DT) // NR
R0 = 4
NSTAGE = NK
NC = DT * BODY
CW = NTILE * W
CS = CW + CW % 2
PIECE = [13, 12, 12, 12]
NPIECE = len(PIECE)
RING = 2
assert PAD_DST >= NP + W and 0 < LAST <= NK // 2 and sum(PIECE) == NTILE and CW <= 3 * 512 and ROUND * W <= 512
assert NR * ROUND == DT * NK and NR * TR == FULL + 1 - DT and NPIECE % RING == 0 and R0 <= NR
assert TR * NK * 4 <= NTILE and BT * P <= 2048 and (TR - 1) * NK + LAST > ROUND // 2

FIRST = [R0 * ROUND // NK, DT, DT, 0]
LAYER_TURNS = [FULL + 1 - f for f in FIRST]
LONE = [LAYER_TURNS[0] - R0 * TR, 0, 0, FULL + 1]
ROUNDS = [R0, NR, NR, 0]
ROUNDS_BEFORE = [sum(ROUNDS[:l]) for l in range(4)]
assert all(n % 2 == 0 for n in ROUNDS)
assert LONE[0] >= DT
BLOCKS_BEFORE = [sum((n - 1) * NK + LAST for n in LAYER_TURNS[:l]) for l in range(5)]
HALVES_BEFORE = [sum(n * 2 for n in LAYER_TURNS[:l]) for l in range(4)]

GROUP = [1, TR, TR, 1]
LAPS = [NK, TR * NK // 2, TR * NK // 2, NK]
assert TR * NK % 2 == 0 and LAPS[1] % 2 == 0


def buffer(l, g, k):
    return (NK * g + k) % LAPS[l]


def fills(l, r, b):
    blocks = [BLOCKS_BEFORE[n + 1] - BLOCKS_BEFORE[n] for n in range(4)]
    earlier = sum(max(0, -(-(blocks[n] - b % LAPS[l]) // LAPS[n])) if b % LAPS[l] < LAPS[n] else 0 for n in range(l))
    return (GROUP[l] * NK // LAPS[l]) * r + (earlier + b // LAPS[l])


def after(eng, sem, value):
    if not isinstance(value, int) or value > 0:
        eng.wait_ge(sem, value)


def turns(eng):
    yield 0, NK
    with eng.Fori(1, FULL) as i:
        yield i, NK
    yield FULL, LAST


def turns_counting(eng):
    yield 0, True
    with eng.Fori(1, DT) as i:
        yield i, True
    with eng.Fori(DT, LONE[0]) as i:
        yield i, False


def rounds(eng, l):
    def turns_of(r, last):
        return [(LONE[l] + TR * r + g, LAST if last and g == TR - 1 else NK) for g in range(TR)]
    yield 0, 0, turns_of(0, False)
    with eng.Fori(0, ROUNDS[l] // 2 - 1) as j:
        for parity in (1, 0):
            r = 2 * j + 2 - parity
            yield r, parity, turns_of(r, False)
    yield ROUNDS[l] - 1, 1, turns_of(ROUNDS[l] - 1, True)


def group_of(l, r, g, m):
    return (m, 0) if GROUP[l] == 1 else (r, g)


def layer_turns(eng, l):
    if l == 3:
        for i, nk in turns(eng):
            yield i, 0, i, nk
        return
    if l == 0:
        for i, _ in turns_counting(eng):
            yield i, 0, i, NK
    for r, _, group in rounds(eng, l):
        for g, (m, nk) in enumerate(group):
            yield *group_of(l, r, g, m), m, nk


def staggered(*stages):
    for at in range(NCH + max(lag for lag, _ in stages)):
        for lag, stage in stages:
            if 0 <= at - lag < NCH:
                c = at - lag
                stage(c, c % 2, JC if c < NCH - 1 else JL)


def gnn_kernel(nc, x, src_t, dst_t, dst_first, edge_T, WlT, bl, WrT, mw1, mb1, uw1, ub1, uw2, ub2, out):
    with ExitStack() as ctx:
        def sb(name, shape, dt=F32):
            return ctx.enter_context(nc.sbuf_tensor(name, shape, dt))

        def sem(name):
            return ctx.enter_context(nc.semaphore(name))

        bank = [ctx.enter_context(nc.psum_tensor(f"bank{b}", [P, 512], F32)) for b in range(8)]
        table = [nc.dram_tensor(f"table{l}", [NP, D], F32).ap() for l in range(4)]
        counts = nc.dram_tensor("counts", [DT * NK, P, CS], F16).ap()

        ident = sb("ident", [P, P])
        ones = sb("ones", [P, P])
        ones_h = sb("ones_h", [P, P], BF16)
        iota_f = sb("iota_f", [P, CH])
        iota_h = sb("iota_h", [P, CW], F16)
        wl = sb("wl", [P, 3, D])
        wr = sb("wr", [P, 3, D])
        mw = sb("mw", [P, 2, D])
        uw = sb("uw", [P, 2, D])
        uw2_sb = sb("uw2_sb", [P, D])
        bcol = sb("bcol", [P, 4])
        mb1_all = sb("mb1_all", [P, 1, D])
        ub2_all = sb("ub2_all", [P, 1, D])
        eps_col = sb("eps_col", [P, 1])

        src_sb = sb("src_sb", [P, (FULL + 1) * BODY], I32)
        first_row = sb("first_row", [1, NB], I32)
        rel = sb("rel", [P, NB, BT])
        left = sb("left", [P, NT])
        key = sb("key", [P, NC])
        low = sb("low", [P, NC])
        left_n = sb("left_n", [P, 1])
        left_flag = sb("left_flag", [P, 1], I32)

        hT = sb("hT", [P, NP])
        acc = sb("acc", [P, 2, NA])
        parts = sb("parts", [P, 3, NCH * JC, D], BF16)

        idx = sb("idx", [P, max(LAPS) // 2, HALF], I32)
        gath = sb("gath", [P, max(LAPS) * BT, D])
        onehot = sb("onehot", [P, NK, BT, W])
        onehot_h = onehot[:, :, :, :].rearrange("p k t w -> p (k t w)").bitcast(BF16).rearrange(
            "p (k t w h) -> p k t w h", k=NK, t=BT, h=2)
        HOT, LOWHOT, STAGE = 2 * BT * CS, 2 * BT * P, NSTAGE * CS
        region = sb("region", [P, HOT + LOWHOT + STAGE], BF16)
        pairhot = region[:, 0:HOT].rearrange("p (k j n) -> p k j n", k=2, j=BT)
        lowhot = region[:, HOT:HOT + LOWHOT].rearrange("p (k j n) -> p k j n", k=2, j=BT)
        stage = region[:, HOT + LOWHOT:].bitcast(F16).rearrange("p (k n) -> p k n", k=NSTAGE)
        ring = region[:, 0:RING * ROUND * PIECE[0] * W].bitcast(F16).rearrange("p (q b n) -> p q b n", q=RING, b=ROUND)
        EF, PRE = 2 * HALF * P, 2 * BT * D
        efT = region[:, 0:2 * EF].bitcast(F32).rearrange("p (q n) -> p q n", q=2)
        pre = region[:, 2 * EF:2 * EF + 2 * PRE].bitcast(F32).rearrange("p (q n) -> p q n", q=2)
        msg = region[:, 2 * EF + 2 * PRE:2 * EF + 4 * PRE].bitcast(F32).rearrange("p (q t d) -> p q t d", q=2, t=BT)
        round_hot = region[:, RING * ROUND * PIECE[0] * W:(RING * PIECE[0] + BT) * ROUND * W].rearrange("p (t n) -> p t n", t=BT)
        scratch = region[:, :].bitcast(I32)
        iota_i = scratch[:, 0:CW]
        dst_i, first_i, src_high, src_low = (scratch[:, at:at + w] for at, w in
                                             [(CW, NT), (CW + NT, NB), (CW + NT + NB, NC), (CW + NT + NB + NC, NC)])
        dense_sum = sb("dense_sum", [P, 2, ROUND * W])

        xin = sb("xin", [P, 2, JC, D])
        stats = sb("stats", [P, 2, JC, 6])
        meanvar = sb("meanvar", [P, 2, JC, 2])
        std = sb("std", [P, 2, JC])
        rstd = sb("rstd", [P, 2, JC])
        shift = sb("shift", [P, 2, JC])
        hn = sb("hn", [P, 2, JC, D])
        z = sb("z", [P, 2, CH])
        rows = sb("rows", [P, 2, JC, D])

        idx_left = sb("idx_left", [P, 1], I32)
        gath_left, ef_left, pre_left, msg_left = (xin[:, 0, j, :] for j in range(4))
        hot_left = z[:, 0, :]

        consts_in = sem("consts_in")
        passed = sem("passed")
        edges_in = sem("edges_in")
        const_built = sem("const_built")
        prep = sem("prep")
        PREP_LEFT = 15
        prep_act = sem("prep_act")
        left_sum = sem("left_sum")
        flag_ready = sem("flag_ready")
        idx_ready = sem("idx_ready")
        gathered = [sem(f"gathered{s}") for s in range(max(LAPS) * BT)]
        onehot_ready = sem("onehot_ready")
        block_summed = sem("block_summed")
        added = sem("added")
        pairhot_ready = sem("pairhot_ready")
        block_counted = sem("block_counted")
        counts_ready = sem("counts_ready")
        counts_out = [sem(f"counts_out{k}") for k in range(NSTAGE)]
        counts_in = [sem(f"counts_in{q}") for q in range(RING)]
        piece_used = sem("piece_used")
        round_hot_ready = sem("round_hot_ready")
        round_copied = sem("round_copied")
        dense_added = sem("dense_added")
        ef_in = [sem("ef_in0"), sem("ef_in1")]
        edge_mm = sem("edge_mm")
        pre_ready = sem("pre_ready")
        msg_ready = sem("msg_ready")
        acc_zeroed = sem("acc_zeroed")
        degree_zeroed = sem("degree_zeroed")
        out_written = [sem("out_written0"), sem("out_written1")]
        table_in = [[sem(f"table_in{l}_{q}") for q in range(2)] for l in range(4)]
        x_chunk_in = [sem(f"x_chunk_in{c}") for c in range(NCH)]
        x_in = [sem("x_in0"), sem("x_in1")]
        LN = ["stats_ready", "var_ready", "std_ready", "rstd_ready", "y_ready", "hn_ready", "turned", "hT_ready"]
        CONV = ["agg_ready", "z_mm", "z_ready", "turned", "rows_ready", "res_ready"]
        PARTS = ["part0_ready", "part1_ready", "rest_ready", "parts_ready"]
        USED = [LN + PARTS, CONV + PARTS, CONV + PARTS, LN + ["agg_ready", "z_mm", "z_ready", "x1_ready", "hn_turned", "row_mm", "rows_ready", "h_added", "ub2_added"],
                ["z_mm", "z_ready", "row_mm", "rows_ready"]]
        USED[1] = USED[1] + ["sums_done", "degree_ready", "inverse_ready"]
        st = [{n: sem(f"n{k}_{n}") for n in names} for k, names in enumerate(USED)]
        LEFT = ["idx", "gathered", "onehot", "summed", "added"]
        lf = [{n: sem(f"left{l}_{n}") for n in LEFT + (["ef_in", "edge_mm", "pre", "msg"] if l == 3 else [])} for l in range(4)]

        def apart(eng):
            eng.sem_inc(passed, 1)

        def cols(c, n):
            return slice(c * CH, c * CH + n * P)

        def node_rows(t, c, n):
            return t[cols(c, n), :].rearrange("(j p) d -> p j d", p=P)

        def by_tile(b, n):
            return bank[b][:, 0:n * P].rearrange("p (j d) -> p j d", j=n)

        def kept(c, n):
            return acc[:, 1, cols(c, n)].rearrange("p (j d) -> p j d", j=n)

        def kept_rows(c, q, n):
            return kept(c, n)

        def hn_rows(c, q, n):
            return hn[:, q, 0:n]

        def rows_rows(c, q, n):
            return rows[:, q, 0:n]

        def count_bank(k, b, w):
            return bank[(2 if k % 2 == 0 else 5) + b][:, 0:w]

        def sum_bank(parity):
            return bank[6 - parity][:, 0:ROUND * W]

        block = ctx.enter_context(nc.Block())

        @block.sync
        def _(sp):
            sp.dma_start(dst_i, dst_t).then_inc(edges_in, 16)
            sp.dma_start(first_i, dst_first.to_broadcast([P, NB])).then_inc(edges_in, 16)
            sp.dma_start(first_row[:, :], dst_first).then_inc(edges_in, 16)
            sp.dma_start(src_sb[:, :], src_t).then_inc(edges_in, 16)

            for c in range(NCH):
                n = JC if c < NCH - 1 else JL
                sp.dma_start(kept(c, n), node_rows(x, c, n)).then_inc(x_chunk_in[c], 16)
            for to, of in [(wl[:, :, :], WlT), (wr[:, :, :], WrT), (mw[:, :, :], mw1.rearrange("(t k) m -> k t m", t=2)),
                           (uw[:, :, :], uw1.rearrange("(t k) m -> k t m", t=2)), (uw2_sb[:, :], uw2),
                           (mb1_all[:, 0, :], mb1.rearrange("(o d) -> o d", o=1).to_broadcast([P, D])),
                           (ub2_all[:, 0, :], ub2.rearrange("(o d) -> o d", o=1).to_broadcast([P, D]))]:
                sp.dma_start(to, of).then_inc(consts_in, 16)
            for k in range(4):
                b = ub1 if k == 3 else bl[k]
                sp.dma_start(bcol[:, k:k + 1], b.rearrange("(d o) -> d o", o=1)).then_inc(consts_in, 16)

            def write_table(l, s, ready, of):
                def stage(c, q, n):
                    sp.wait_ge(s[ready], c + 1)
                    sp.dma_start(node_rows(table[l], c, n), of(c, q, n)).then_inc(table_in[l][q], 16)
                return stage

            staggered((0, write_table(0, st[0], "hn_ready", kept_rows)))

            def load_piece(l, r, p):
                at, w = sum(PIECE[:p]), PIECE[p]
                after(sp, piece_used, NPIECE * (ROUNDS_BEFORE[l] + r) + p - RING + 1)
                sp.dma_start(ring[:, p % RING, :, 0:w * W],
                             counts[bass.ds(ROUND * r, ROUND), :, at * W:(at + w) * W].rearrange("b p n -> p b n")
                             ).then_inc(counts_in[p % RING], 16)

            def load_edges(i, nk, q):
                w = min(HALF, nk * BT - q * HALF) * P
                after(sp, edge_mm, NK * (i - 1) + NK // 2 * (q + 1))
                sp.dma_start(efT[:, q, 0:w], edge_T[:, bass.ds((i * 2 + q) * HALF * P, w)]).then_inc(ef_in[q], 16)

            for l in range(4):
                if l == 0:
                    for i, counting in turns_counting(sp):
                        for k in range(NK if counting else 0):
                            sp.wait_ge(counts_ready, NK * i + k + 1)
                            sp.dma_start(counts[bass.ds(NK * i + k, 1), :, 0:CW].rearrange("o p n -> (o p) n"),
                                         stage[:, k, 0:CW]).then_inc(counts_out[k], 16)
                    for k in range(NK):
                        sp.wait_ge(counts_out[k], 16 * DT)
                if l < 3:
                    for r, _, _ in rounds(sp, l):
                        for p in range(NPIECE):
                            if not (l > 0 and isinstance(r, int) and r == 0 and p < RING):
                                load_piece(l, r, p)
                else:
                    for i, nk in turns(sp):
                        for q in range(-(-nk * BT // HALF)):
                            if not isinstance(i, int) or i > 0:
                                load_edges(i, nk, q)
                sp.wait_ge(flag_ready, 1)
                n_left = sp.value_load(left_flag[0:1, 0:1], min_val=0, max_val=EP)
                with sp.If(n_left > 0):
                    s = lf[l]
                    with sp.Fori(0, NT) as t:
                        sp.wait_ge(s["added"], NCH * t + 1)
                        apart(sp)
                        sp.dma_start(idx_left[:, :], src_t[:, bass.ds(t, 1)],
                                     allow_slow_non_contiguous=True).then_inc(s["idx"], 16)
                        if l == 3:
                            sp.dma_start(ef_left, edge_T[:, bass.ds(t * P, P)]).then_inc(s["ef_in"], 16)
                    sp.wait_ge(s["added"], NCH * NT + 1)
                if l < 2:
                    for p in range(RING):
                        load_piece(l + 1, 0, p)
                elif l == 2:
                    sp.wait_ge(piece_used, NPIECE * ROUNDS_BEFORE[3])
                    for q in range(2):
                        load_edges(0, NK, q)
                if l < 2:
                    staggered((0, write_table(l + 1, st[l + 1], "rows_ready", rows_rows)))
                elif l == 2:
                    def load_x(c, q, n):
                        after(sp, st[3]["x1_ready"], c - 1)
                        sp.dma_start(xin[:, q, 0:n], node_rows(x, c, n)).then_inc(x_in[q], 16)

                    staggered((9, write_table(3, st[3], "rows_ready", rows_rows)), (0, load_x))

            def write_out(c, q, n):
                sp.wait_ge(st[4]["rows_ready"], c + 1)
                sp.dma_start(node_rows(out, c, n), rows[:, q, 0:n]).then_inc(out_written[q], 16)

            staggered((0, write_out))
            sp.wait_ge(out_written[0], 16 * -(-NCH // 2))
            sp.wait_ge(out_written[1], 16 * (NCH // 2))

        @block.gpsimd
        def _(pool):
            nc.gpsimd.memset(ident[:, :], 0.0).then_inc(const_built, 1)
            nc.gpsimd.memset(ones[:, :], 1.0).then_inc(const_built, 1)
            nc.gpsimd.memset(ones_h[:, :], 1.0)
            nc.gpsimd.memset(eps_col[:, :], EPS).then_inc(const_built, 1)
            nc.gpsimd.iota(iota_i, pattern=[[1, CW]], base=0, channel_multiplier=0).then_inc(const_built, 1)
            pool.wait_ge(const_built, 4)
            nc.gpsimd.affine_select(out=ident[:, :], in_=ident[:, :], compare_op=ALU.not_equal, fill=1.0, base=0,
                                    pattern=[[-1, P]], channel_multiplier=1).then_inc(const_built, 1)

            nc.gpsimd.memset(acc[:, 0, :], 0.0).then_inc(acc_zeroed, NCH)

            def first_rest(s, of, to):
                def stage(c, q, n):
                    pool.wait_ge(s["part0_ready"], c + 1)
                    after(pool, s["parts_ready"], c - 1)
                    after(pool, s["part1_ready"], c - 1)
                    nc.gpsimd.tensor_tensor(to[:, q, 0:n], of(c, q, n), parts[:, 0, c * JC:c * JC + n, :], ALU.subtract).then_inc(s["rest_ready"], 1)
                return stage

            def third_part(s, of):
                def stage(c, q, n):
                    pool.wait_ge(s["part1_ready"], c + 1)
                    nc.gpsimd.tensor_tensor(parts[:, 2, c * JC:c * JC + n, :], of[:, q, 0:n], parts[:, 1, c * JC:c * JC + n, :],
                                            ALU.subtract).then_inc(s["parts_ready"], 1)
                return stage

            def zero(s):
                def stage(c, q, n):
                    pool.wait_ge(s["z_mm"], c + 1)
                    end = NA if c == NCH - 1 else (c + 1) * CH
                    nc.gpsimd.memset(acc[:, 0, c * CH:end], 0.0).then_inc(acc_zeroed, 1)
                return stage

            def add_h(c, q, n):
                pool.wait_ge(st[3]["hn_ready"], c + 1)
                nc.gpsimd.tensor_tensor(kept(c, n), kept(c, n), hn[:, q, 0:n], ALU.add).then_inc(st[3]["h_added"], 1)

            def add_ub2(c, q, n):
                pool.wait_ge(st[3]["h_added"], c + 1)
                nc.gpsimd.tensor_tensor(kept(c, n), kept(c, n), ub2_all[:, :, :].to_broadcast([P, n, D]), ALU.add).then_inc(st[3]["ub2_added"], 1)

            def at_least_one(c, q, n):
                if c == 0:
                    pool.wait_ge(st[1]["sums_done"], 1)
                to = acc[:, 1, cols(c, n)]
                nc.gpsimd.tensor_scalar(to, to, 1.0, None, ALU.max).then_inc(st[1]["degree_ready"], 1)

            for l in range(4):
                if l == 0:
                    staggered((1, third_part(st[0], rows)), (0, first_rest(st[0], kept_rows, rows)))
                elif l == 3:
                    staggered((5, add_ub2), (4, add_h), (0, zero(st[3])))
                elif l == 1:
                    staggered((11, third_part(st[1], hn)), (9, first_rest(st[1], rows_rows, hn)), (8, zero(st[1])), (0, at_least_one))
                else:
                    staggered((3, third_part(st[l], hn)), (0, zero(st[l])))
                pool.wait_ge(table_in[l][0], 16 * -(-NCH // 2))
                pool.wait_ge(table_in[l][1], 16 * (NCH // 2))
                for r, g, m, nk in layer_turns(pool, l):
                    for t in range(nk * BT):
                        k = t // BT
                        at = buffer(l, g, k) * BT + t % BT
                        half = buffer(l, g, k) // 2
                        if t % HALF == 0:
                            pool.wait_ge(idx_ready, HALVES_BEFORE[l] + 2 * m + t // HALF + 1)
                        if t % BT == 0:
                            if l == 3:
                                after(pool, pre_ready, NK * (m - 1) + k + 1)
                            elif isinstance(m, int):
                                after(pool, block_summed, BLOCKS_BEFORE[l] + max(0, NK * m + k + 1 - LAPS[l]))
                            else:
                                pool.wait_ge(block_summed, BLOCKS_BEFORE[l] + NK * m + k + 1 - LAPS[l])
                            apart(pool)
                        pool.indirect_dma_start(
                            out=gath[:, at, :], out_offset=None, in_=table[l],
                            in_offset=bass.IndirectOffsetOnAxis(ap=idx[:, half, t % HALF:t % HALF + 1].bitcast(U32), axis=0),
                        ).then_inc(gathered[at], 16)
                pool.wait_ge(flag_ready, 1)
                n_left = pool.value_load(left_flag[0:1, 0:1], min_val=0, max_val=EP)
                with pool.If(n_left > 0):
                    s = lf[l]
                    with pool.Fori(0, NT) as t:
                        pool.wait_ge(s["idx"], 16 * t + 16)
                        apart(pool)
                        pool.indirect_dma_start(
                            out=gath_left, out_offset=None, in_=table[l],
                            in_offset=bass.IndirectOffsetOnAxis(ap=idx_left[:, 0:1].bitcast(U32), axis=0),
                        ).then_inc(s["gathered"], 16)

        @block.scalar
        def _(act):
            act.wait_ge(const_built, 5)
            nc.scalar.copy(iota_h[:, :], iota_i).then_inc(prep_act, 1)

            def indices(l, r, q, g=0):
                for k in (2 * q, 2 * q + 1):
                    for j in range(BT):
                        after(act, gathered[buffer(l, g, k) * BT + j], 16 * fills(l, r, NK * g + k))
                if isinstance(r, int) and r == 0:
                    after(act, idx_ready, HALVES_BEFORE[l])
                turn = FIRST[l] + GROUP[l] * r + g
                nc.scalar.copy(idx[:, buffer(l, g, 2 * q) // 2, :], src_sb[:, bass.ds((turn * 2 + q) * HALF, HALF)]).then_inc(idx_ready, 1)

            def last_turn(l, m):
                return isinstance(m, int) and m == LAYER_TURNS[l] - 1

            def deviation(s):
                def stage(c, q, n):
                    act.wait_ge(s["var_ready"], c + 1)
                    nc.scalar.activation(std[:, q, 0:n], meanvar[:, q, 0:n, 1], ACT.Sqrt, bias=eps_col[:, 0:1]).then_inc(s["std_ready"], 1)
                return stage

            def positive(c, q, n):
                act.wait_ge(st[0]["y_ready"], c + 1)
                nc.scalar.activation(kept(c, n), kept(c, n), ACT.Relu).then_inc(st[0]["hn_ready"], 1)

            def features(s, turned, b):
                def stage(c, q, n):
                    act.wait_ge(s[turned], c + 1)
                    nc.scalar.copy(hT[:, cols(c, n)], bank[b + q][:, 0:n * P]).then_inc(s["hT_ready"], 1)
                return stage

            def second_part(s, of):
                def stage(c, q, n):
                    act.wait_ge(s["rest_ready"], c + 1)
                    nc.scalar.copy(parts[:, 1, c * JC:c * JC + n, :], of[:, q, 0:n]).then_inc(s["part1_ready"], 1)
                return stage

            def first_part(c, q, n):
                act.wait_ge(st[0]["hn_ready"], c + 1)
                nc.scalar.copy(parts[:, 0, c * JC:c * JC + n, :], kept(c, n)).then_inc(st[0]["part0_ready"], 1)

            act.wait_ge(edges_in, 64)
            for q in range(2):
                indices(0, 0, q)
            staggered((0, deviation(st[0])), (1, positive), (2, first_part), (2, features(st[0], "turned", 2)),
                      (3, second_part(st[0], rows)))
            act.wait_ge(consts_in, 16 * 11)

            def drain_round(l, r, parity):
                ordinal = ROUNDS_BEFORE[l] + r
                act.wait_ge(piece_used, NPIECE * (ordinal + 1))
                after(act, dense_added, ROUND * ordinal)
                if l == 0:
                    nc.scalar.copy(dense_sum[:, 1, :], bank[7][:, 0:ROUND * W])
                nc.scalar.copy(dense_sum[:, 0, :], sum_bank(parity)).then_inc(round_copied, 1)

            for l in range(4):
                if l == 0:
                    for i, counting in turns_counting(act):
                        for k in range(NK):
                            if counting:
                                act.wait_ge(block_counted, NK * i + k + 1)
                                after(act, counts_out[k], 16 * i)
                                for b in range(3):
                                    w = min(512, CW - b * 512)
                                    m = nc.scalar.copy(stage[:, k, b * 512:b * 512 + w], count_bank(k, b, w))
                                m.then_inc(counts_ready, 1)
                            if k % 2 == 0:
                                indices(0, i + 1, k // 2)
                if l < 3:
                    for r, parity, group in rounds(act, l):
                        for g, (m, nk) in enumerate(group):
                            for q in range(2):
                                if g == 0 and q == (l > 0) and not (isinstance(r, int) and r == 0):
                                    drain_round(l, r - 1, 1 - parity)
                                if not last_turn(l, m):
                                    of, turn = group_of(l, r + (g + 1) // TR, (g + 1) % TR, m + 1)
                                    indices(l, of, q, turn)
                    drain_round(l, ROUNDS[l] - 1, 1)
                else:
                    for i, nk in turns(act):
                        for k in range(nk):
                            act.wait_ge(pre_ready, NK * i + k + 1)
                            after(act, block_summed, BLOCKS_BEFORE[3] + NK * i + k - 1)
                            nc.scalar.activation(msg[:, k % 2], pre[:, k % 2].rearrange("p (t d) -> p t d", t=BT),
                                                 ACT.Silu).then_inc(msg_ready, 1)
                            if k % 2 == 1:
                                indices(3, i + 1, k // 2)
                if l < 3:
                    for q in range(2):
                        indices(l + 1, 0, q)
                if l == 3:
                    act.wait_ge(flag_ready, 1)
                    n_left = act.value_load(left_flag[0:1, 0:1], min_val=0, max_val=EP)
                    with act.If(n_left > 0):
                        s = lf[3]
                        with act.Fori(0, NT) as t:
                            act.wait_ge(s["pre"], t + 1)
                            nc.scalar.activation(msg_left, pre_left, ACT.Silu).then_inc(s["msg"], 1)
                elif l < 2:
                    s = st[l + 1]

                    def convolved(c, q, n):
                        act.wait_ge(s["z_mm"], c + 1)
                        to = hT[:, cols(c, n)] if l == 0 else z[:, q, 0:n * P]
                        if l == 1:
                            after(act, s["res_ready"], c - 1)
                        nc.scalar.activation(to, bank[q][:, 0:n * P], ACT.Relu, bias=bcol[:, l:l + 1]).then_inc(s["z_ready"], 1)

                    def by_rows(c, q, n):
                        act.wait_ge(s["turned"], c + 1)
                        after(act, table_in[l + 1][q], 16 * (c // 2))
                        after(act, s["rest_ready"], c - 1)
                        nc.scalar.copy(rows[:, q, 0:n], by_tile(2 + q, n)).then_inc(s["rows_ready"], 1)
                        nc.scalar.copy(parts[:, 0, c * JC:c * JC + n, :], by_tile(2 + q, n)).then_inc(s["part0_ready"], 1)

                    staggered((4, second_part(s, hn)), (2, by_rows), (0, convolved))
                else:
                    s = st[3]

                    def convolved(c, q, n):
                        act.wait_ge(s["z_mm"], c + 1)
                        after(act, s["turned"], c - 1)
                        nc.scalar.activation(z[:, q, 0:n * P], bank[q][:, 0:n * P], ACT.Identity, bias=bcol[:, 2:3]).then_inc(s["z_ready"], 1)

                    def normalised(c, q, n):
                        act.wait_ge(s["y_ready"], c + 1)
                        after(act, s["hn_turned"], c - 1)
                        after(act, s["h_added"], c - 1)
                        for j in range(n):
                            m = nc.scalar.activation(hn[:, q, j, :], kept(c, n)[:, j, :], ACT.Relu, scale=rstd[:, q, j:j + 1], bias=shift[:, q, j:j + 1])
                        m.then_inc(s["hn_ready"], 1)

                    staggered((7, features(s, "hn_turned", 4)), (5, normalised), (4, deviation(s)), (0, convolved))
            s = st[4]

            def updated(c, q, n):
                act.wait_ge(s["z_mm"], c + 1)
                after(act, s["row_mm"], c - 1)
                nc.scalar.activation(z[:, q, 0:n * P], bank[q][:, 0:n * P], ACT.Silu, bias=bcol[:, 3:4]).then_inc(s["z_ready"], 1)

            staggered((0, updated))

        @block.tensor
        def _(pe):
            pe.wait_ge(const_built, 5)

            def turn_rows(s, of, turned, b):
                def stage(c, q, n):
                    pe.wait_ge(s["hn_ready"], c + 1)
                    after(pe, s["hT_ready"], c - 1)
                    for j in range(n):
                        m = nc.tensor.transpose(bank[b + q][:, j * P:(j + 1) * P], of(c, q, n)[:, j, :], ident[:, :])
                    m.then_inc(s[turned], 1)
                return stage

            staggered((0, turn_rows(st[0], kept_rows, "turned", 2)))
            pe.wait_ge(st[0]["hT_ready"], NCH)
            pe.wait_ge(prep, PREP_LEFT)
            nc.tensor.matmul(bank[7][:, 0:1], ones[:, :], left_n[:, :], start=True, stop=True).then_inc(left_sum, 1)
            pe.wait_ge(consts_in, 16 * 11)
            pe.wait_ge(flag_ready, 1)

            def sum_block(l, r, g, m, k, rows_of):
                done = BLOCKS_BEFORE[l] + NK * m + k
                pe.wait_ge(onehot_ready, done + 1)
                after(pe, added, done - 1)
                for j in range(BT):
                    t = BT * buffer(l, g, k) + j
                    if l < 3:
                        pe.wait_ge(gathered[t], 16 * fills(l, r, NK * g + k) + 16)
                    mm = nc.tensor.matmul(bank[k % 2][:, 0:W], rows_of(t), onehot[:, k, j, :], start=(j == 0), stop=(j == BT - 1))
                if l == 0:
                    for j in range(BT):
                        mm = nc.tensor.matmul(bank[k % 2][:, W:2 * W], ones_h[:, :], onehot_h[:, k, j, :, 1], start=(j == 0), stop=(j == BT - 1))
                mm.then_inc(block_summed, 1)

            def count_block(o, n):
                pe.wait_ge(pairhot_ready, o + 1)
                after(pe, counts_ready, o - 1)
                for j in range(BT):
                    for b in range(3):
                        w = min(512, CW - b * 512)
                        mm = nc.tensor.matmul(count_bank(n, b, w), lowhot[:, n % 2, j, :], pairhot[:, n % 2, j, b * 512:b * 512 + w],
                                              start=(j == 0), stop=(j == BT - 1))
                mm.then_inc(block_counted, 1)

            def edge_products(i, k):
                done = NK * i + k
                if k % 2 == 0:
                    pe.wait_ge(ef_in[k // 2], 16 * i + 16)
                after(pe, pre_ready, done - 1)
                for j in range(BT):
                    t = (k % 2) * BT + j
                    mm = nc.tensor.matmul(bank[4 + k % 2][:, j * D:(j + 1) * D], efT[:, k // 2, t * P:(t + 1) * P],
                                          mw[:, 1, :], start=True, stop=True)
                mm.then_inc(edge_mm, 1)

            for l in range(4):
                if l == 0:
                    for i, counting in turns_counting(pe):
                        for k in range(NK):
                            sum_block(0, i, 0, i, k, lambda t: gath[:, t, :])
                            if counting:
                                count_block(NK * i + k, k)
                if l < 3:
                    for r, parity, group in rounds(pe, l):
                        blocks = [(*group_of(l, r, g, m), m, k) for g, (m, nk) in enumerate(group) for k in range(nk)]
                        ordinal = ROUNDS_BEFORE[l] + r
                        hi = 0
                        for p, w in enumerate(PIECE):
                            for h in range(w):
                                if hi % 4 == 0 and 0 < hi // 4 <= len(blocks):
                                    sum_block(l, *blocks[hi // 4 - 1], lambda t: gath[:, t, :])
                                if h == 0:
                                    pe.wait_ge(counts_in[p % RING], 16 * (NPIECE // RING * ordinal + p // RING + 1))
                                if hi == 0:
                                    after(pe, round_copied, ordinal - 1)
                                if hi % JC == 0 and isinstance(r, int) and r == 0:
                                    pe.wait_ge(st[l]["parts_ready"], hi // JC + 1)
                                for a in range(3):
                                    mm = nc.tensor.matmul(sum_bank(parity).rearrange("p (b n) -> p b n", b=ROUND), parts[:, a, hi, :],
                                                          ring[:, p % RING, :, h * W:(h + 1) * W],
                                                          start=(hi == 0 and a == 0), stop=(hi == NTILE - 1 and a == 2))
                                hi += 1
                            mm.then_inc(piece_used, 1)
                            if l == 0 and p == 0:
                                pe.wait_ge(round_hot_ready, r + 1)
                                after(pe, round_copied, ordinal)
                                for j in range(BT):
                                    mm = nc.tensor.matmul(bank[7][:, 0:ROUND * W], ones_h[:, :], round_hot[:, j, :], start=(j == 0), stop=(j == BT - 1))
                else:
                    for i, nk in turns(pe):
                        edge_products(i, 0)
                        for k in range(nk):
                            if k + 1 < nk:
                                edge_products(i, k + 1)
                            pe.wait_ge(msg_ready, NK * i + k + 1)
                            sum_block(3, i, 0, i, k, lambda t: msg[:, (t // BT) % 2, t % BT, :])
                n_left = pe.value_load(left_flag[0:1, 0:1], min_val=0, max_val=EP)
                with pe.If(n_left > 0):
                    s = lf[l]
                    with pe.Fori(0, NT) as t:
                        if l == 3:
                            pe.wait_ge(s["ef_in"], 16 * t + 16)
                            nc.tensor.matmul(bank[5][:, 0:D], ef_left, mw[:, 1, :], start=True, stop=True).then_inc(s["edge_mm"], 1)
                            pe.wait_ge(s["msg"], t + 1)
                        else:
                            pe.wait_ge(s["gathered"], 16 * t + 16)
                        for c in range(NCH):
                            w = min(CH, NP - c * CH)
                            pe.wait_ge(s["onehot"], NCH * t + c + 1)
                            mm = nc.tensor.matmul(bank[4][:, 0:w], gath_left if l < 3 else msg_left, hot_left[:, 0:w],
                                                  start=True, stop=True)
                            if l == 0:
                                mm = nc.tensor.matmul(bank[5][:, 0:w], ones[:, :], hot_left[:, 0:w], start=True, stop=True)
                            mm.then_inc(s["summed"], 1)
                    pe.wait_ge(s["added"], NCH * NT + 1)
                if l == 3:
                    break
                s = st[l + 1]

                def convolve(c, q, n):
                    pe.wait_ge(s["agg_ready"], c + 1)
                    after(pe, s["z_ready"], c - 1)
                    nc.tensor.matmul(bank[q][:, 0:n * P], wl[:, l, :], acc[:, 0, cols(c, n)], start=True, stop=False)
                    nc.tensor.matmul(bank[q][:, 0:n * P], wr[:, l, :], hT[:, cols(c, n)], start=False, stop=True).then_inc(s["z_mm"], 1)

                def turn_features(c, q, n):
                    pe.wait_ge(s["res_ready"] if l == 1 else s["z_ready"], c + 1)
                    after(pe, s["part0_ready"] if l < 2 else s["x1_ready"], c - 1)
                    for j in range(n):
                        of = z[:, q, j * P:(j + 1) * P] if l == 2 else hT[:, c * CH + j * P:c * CH + (j + 1) * P]
                        mm = nc.tensor.transpose(bank[2 + q][:, j * P:(j + 1) * P], of, ident[:, :])
                    mm.then_inc(s["turned"], 1)

                def message_rows(c, q, n):
                    pe.wait_ge(s["hT_ready"], c + 1)
                    after(pe, s["rows_ready"], c - 1)
                    for j in range(n):
                        to = bank[6 + q][:, j * P:(j + 1) * P]
                        mm = nc.tensor.matmul(to, hT[:, c * CH + j * P:c * CH + (j + 1) * P], mw[:, 0, :], start=True, stop=True)
                    mm.then_inc(s["row_mm"], 1)

                if l < 2:
                    staggered((2, turn_features), (0, convolve))
                else:
                    staggered((8, message_rows), (6, turn_rows(s, hn_rows, "hn_turned", 4)), (2, turn_features), (0, convolve))
                    pe.wait_ge(s["hT_ready"], NCH)
            s = st[4]
            pe.wait_ge(added, BLOCKS_BEFORE[4])

            def update(c, q, n):
                after(pe, s["z_ready"], c - 1)
                nc.tensor.matmul(bank[q][:, 0:n * P], uw[:, 0, :], hT[:, cols(c, n)], start=True, stop=False)
                nc.tensor.matmul(bank[q][:, 0:n * P], uw[:, 1, :], acc[:, 0, cols(c, n)], start=False, stop=True).then_inc(s["z_mm"], 1)

            def update_rows(c, q, n):
                pe.wait_ge(s["z_ready"], c + 1)
                after(pe, s["rows_ready"], c - 1)
                for j in range(n):
                    to = bank[2 + q][:, j * P:(j + 1) * P]
                    mm = nc.tensor.matmul(to, z[:, q, j * P:(j + 1) * P], uw2_sb[:, :], start=True, stop=True)
                mm.then_inc(s["row_mm"], 1)

            staggered((2, update_rows), (0, update))

        @block.vector
        def _(dve):
            dve.wait_ge(const_built, 5)
            nc.vector.tensor_copy(iota_f[:, :], iota_i[:, 0:CH])

            def statistics(s, before):
                def stage(c, q, n):
                    before(c, q, n)
                    of = kept(c, n)
                    for j in range(n):
                        m = nc.vector.bn_stats(stats[:, q, j, :], of[:, j, :])
                    m.then_inc(s["stats_ready"], 1)
                    dve.wait_ge(s["stats_ready"], c + 1)
                    after(dve, s["std_ready"], c - 1)
                    for j in range(n):
                        m = nc.vector.bn_aggr(meanvar[:, q, j, :], stats[:, q, j, :])
                    m.then_inc(s["var_ready"], 1)
                return stage

            def normalise(c, q, n):
                s = st[0]
                dve.wait_ge(s["std_ready"], c + 1)
                nc.vector.reciprocal(rstd[:, q, 0:n], std[:, q, 0:n]).then_inc(s["rstd_ready"], 1)
                dve.wait_ge(s["rstd_ready"], c + 1)
                for j in range(n):
                    to = kept(c, n)[:, j, :]
                    m = nc.vector.tensor_scalar(to, to, meanvar[:, q, j, 0:1], rstd[:, q, j:j + 1], ALU.subtract, ALU.mult)
                m.then_inc(s["y_ready"], 1)

            def x_loaded(c, q, n):
                dve.wait_ge(x_chunk_in[c], 16)

            def first_rest(s, of, to):
                def stage(c, q, n):
                    dve.wait_ge(s["part0_ready"], c + 1)
                    after(dve, s["parts_ready"], c - 1)
                    after(dve, s["part1_ready"], c - 1)
                    nc.vector.tensor_tensor(to[:, q, 0:n], of(c, q, n), parts[:, 0, c * JC:c * JC + n, :], ALU.subtract).then_inc(s["rest_ready"], 1)
                return stage

            staggered((1, normalise), (0, statistics(st[0], x_loaded)))

            dve.wait_ge(edges_in, 64)
            steps = [0]

            def step(ins):
                steps[0] += 1
                ins.then_inc(prep, 1)
                dve.wait_ge(prep, steps[0])

            dst_b = dst_i.rearrange("p (b t) -> p b t", t=BT)
            first_b = first_i.rearrange("p (b o) -> p b o", o=1).to_broadcast([P, NB, BT])
            rel_f = rel[:, :, :].rearrange("p b t -> p (b t)")
            outside = xin[:, :, :, :].rearrange("p q j d -> p (q j d)")[:, 0:NT]
            real = z[:, :, :].rearrange("p q n -> p (q n)")[:, 0:NT]
            step(nc.vector.tensor_tensor(rel[:, :, :], dst_b, first_b, ALU.subtract))
            step(nc.vector.tensor_scalar(outside, rel_f, 0.0, None, ALU.is_lt))
            step(nc.vector.tensor_scalar(real, dst_i, float(N), None, ALU.is_lt))
            step(nc.vector.scalar_tensor_tensor(out=outside, in0=rel_f, scalar=float(W), in1=outside, op0=ALU.is_ge, op1=ALU.add))
            step(nc.vector.tensor_scalar(src_high, src_sb[:, 0:NC], 7, None, ALU.arith_shift_right))
            step(nc.vector.tensor_scalar(src_low, src_sb[:, 0:NC], P - 1, None, ALU.bitwise_and))
            step(nc.vector.tensor_copy(low[:, :], src_low))
            step(nc.vector.scalar_tensor_tensor(out=key[:, :], in0=src_high, scalar=float(W), in1=rel_f[:, 0:NC], op0=ALU.mult, op1=ALU.add))
            step(nc.vector.tensor_scalar(left[:, 0:NC], outside[:, 0:NC], -1.0, 1.0, ALU.mult, ALU.add))
            step(nc.vector.scalar_tensor_tensor(out=key[:, :], in0=key[:, :], scalar=1.0, in1=left[:, 0:NC], op0=ALU.add, op1=ALU.mult))
            step(nc.vector.tensor_scalar(key[:, :], key[:, :], -1.0, None, ALU.add))
            step(nc.vector.tensor_tensor(outside, outside, real, ALU.mult))
            step(nc.vector.scalar_tensor_tensor(out=left[:, :], in0=dst_i, scalar=1.0, in1=outside, op0=ALU.add, op1=ALU.mult))
            step(nc.vector.tensor_scalar(left[:, :], left[:, :], -1.0, None, ALU.add))
            step(nc.vector.reduce_sum(left_n[:, :], outside, AX_X))
            assert steps[0] == PREP_LEFT
            dve.wait_ge(left_sum, 1)
            nc.vector.tensor_copy(left_flag[:, :], bank[7][:, 0:1]).then_inc(flag_ready, 1)
            dve.wait_ge(flag_ready, 1)
            dve.wait_ge(prep_act, 1)
            iota_w = iota_f[:, 0:W].rearrange("p (o w) -> p o w", o=1).to_broadcast([P, BT, W])

            for l in range(4):
                R = 2 if l == 0 else 1
                if l == 0:
                    for q in range(2):
                        dve.wait_ge(table_in[0][q], 16 * -(-(NCH - q) // 2))
                    dve.wait_ge(st[0]["turned"], NCH)
                    dve.wait_ge(st[0]["rest_ready"], NCH)
                    nc.vector.memset(acc[:, 1, :], 0.0).then_inc(degree_zeroed, 1)
                    dve.wait_ge(degree_zeroed, 1)

                def hot(m, k, turn):
                    first = isinstance(m, int) and m == 0
                    after(dve, block_summed, BLOCKS_BEFORE[l] + (0 if first else NK * (m - 1) + k + 1))
                    b = rel[:, bass.ds(NK * turn + k, 1), :].rearrange("p o t -> p t o").to_broadcast([P, BT, W])
                    nc.vector.tensor_tensor(onehot[:, k], iota_w, b, ALU.is_equal).then_inc(onehot_ready, 1)

                def add(m, k, turn):
                    if k == 0 and isinstance(m, int) and m == 0:
                        dve.wait_ge(acc_zeroed, NCH * (l + 1))
                    done = BLOCKS_BEFORE[l] + NK * m + k
                    w0 = dve.value_load(first_row[0:1, bass.ds(NK * turn + k, 1)], min_val=0, max_val=N - 1)
                    dve.wait_ge(block_summed, done + 1)
                    after(dve, added, done)
                    to = acc[:, 0:R, bass.ds(w0, W)]
                    nc.vector.tensor_tensor(to, to, bank[k % 2][:, 0:R * W].rearrange("p (r w) -> p r w", r=R), ALU.add).then_inc(added, 1)

                def add_dense(r, windows, before):
                    ordinal = ROUND * (ROUNDS_BEFORE[l] + r) + windows[0]
                    w0 = [dve.value_load(first_row[0:1, bass.ds(ROUND * r + b, 1)], min_val=0, max_val=N - 1) for b in windows]
                    dve.wait_ge(round_copied, ROUNDS_BEFORE[l] + r + 1)
                    dve.wait_ge(added, before)
                    for n, b in enumerate(windows):
                        after(dve, dense_added, ordinal + n)
                        to = acc[:, 0:R, bass.ds(w0[n], W)]
                        nc.vector.tensor_tensor(to, to, dense_sum[:, 0:R, b * W:(b + 1) * W], ALU.add).then_inc(dense_added, 1)
                    dve.wait_ge(dense_added, ordinal + len(windows))

                def pair_hot(o, n):
                    after(dve, block_counted, o - 1)
                    for j in range(BT):
                        t = bass.ds(BT * o + j, 1)
                        nc.vector.tensor_scalar(lowhot[:, n % 2, j, :], iota_h[:, 0:P], low[:, t], None, ALU.is_equal)
                        m = nc.vector.tensor_scalar(pairhot[:, n % 2, j, 0:CW], iota_h[:, :], key[:, t], None, ALU.is_equal)
                    m.then_inc(pairhot_ready, 1)

                def add_features(i, k):
                    done = NK * i + k
                    dve.wait_ge(edge_mm, done + 1)
                    for j in range(BT):
                        dve.wait_ge(gathered[BT * k + j], 16 * fills(3, i, k) + 16)
                    after(dve, msg_ready, done - 1)
                    nc.vector.tensor_tensor(pre[:, k % 2], bank[4 + k % 2][:, 0:BT * D],
                                            gath[:, BT * k:BT * (k + 1), :].rearrange("p t d -> p (t d)"), ALU.add).then_inc(pre_ready, 1)

                def hot_round(r):
                    after(dve, piece_used, NPIECE * (r - 1) + 2)
                    iota_r = iota_f[:, 0:W].rearrange("p (o w) -> p o w", o=1).to_broadcast([P, ROUND, W])
                    for j in range(BT):
                        b = rel[:, bass.ds(ROUND * r, ROUND), j:j + 1].to_broadcast([P, ROUND, W])
                        m = nc.vector.tensor_tensor(round_hot[:, j, :].rearrange("p (b w) -> p b w", b=ROUND), iota_r, b, ALU.is_equal)
                    m.then_inc(round_hot_ready, 1)

                if l == 0:
                    for i, counting in turns_counting(dve):
                        for k in range(NK):
                            hot(i, k, i + FIRST[0])
                            if k:
                                add(i, k - 1, i + FIRST[0])
                            if counting:
                                pair_hot(NK * i + k, k)
                        add(i, NK - 1, i + FIRST[0])
                    for k in range(NK):
                        dve.wait_ge(counts_out[k], 16 * DT)
                if l < 3:
                    for r, _, group in rounds(dve, l):
                        blocks = [(m, k) for m, nk in group for k in range(nk)]
                        if l == 0:
                            hot_round(r)
                        for n, (m, k) in enumerate(blocks):
                            hot(m, k, m + FIRST[l])
                            if n:
                                add(*blocks[n - 1], blocks[n - 1][0] + FIRST[l])
                            if 1 <= n <= ROUND // 2 and not (isinstance(r, int) and r == 0):
                                before = BLOCKS_BEFORE[l] + NK * (LONE[l] + TR * r) + n
                                add_dense(r - 1, (2 * n - 2, 2 * n - 1), before)
                        add(*blocks[-1], blocks[-1][0] + FIRST[l])
                    add_dense(ROUNDS[l] - 1, range(ROUND), BLOCKS_BEFORE[l + 1])
                else:
                    for i, nk in turns(dve):
                        for k in range(nk):
                            hot(i, k, i)
                            add_features(i, k)
                            if k:
                                add(i, k - 1, i)
                        add(i, nk - 1, i)

                n_left = dve.value_load(left_flag[0:1, 0:1], min_val=0, max_val=EP)
                dve.wait_ge(added, BLOCKS_BEFORE[l + 1])
                with dve.If(n_left > 0):
                    s = lf[l]
                    nc.vector.memset(hot_left, 0.0).then_inc(s["added"], 1)
                    with dve.Fori(0, NT) as t:
                        if l == 3:
                            dve.wait_ge(s["edge_mm"], t + 1)
                            dve.wait_ge(s["gathered"], 16 * t + 16)
                            nc.vector.tensor_tensor(pre_left, bank[5][:, 0:D], gath_left, ALU.add).then_inc(s["pre"], 1)
                        for c in range(NCH):
                            w = min(CH, NP - c * CH)
                            dve.wait_ge(s["added"], NCH * t + c + 1)
                            nc.vector.tensor_scalar(hot_left, iota_f[:, :], float(CH * c), left[:, bass.ds(t, 1)],
                                                    ALU.add, ALU.is_equal).then_inc(s["onehot"], 1)
                            dve.wait_ge(s["summed"], NCH * t + c + 1)
                            to = acc[:, 0, c * CH:c * CH + w]
                            m = nc.vector.tensor_tensor(to, to, bank[4][:, 0:w], ALU.add)
                            if l == 0:
                                to = acc[:, 1, c * CH:c * CH + w]
                                m = nc.vector.tensor_tensor(to, to, bank[5][:, 0:w], ALU.add)
                            m.then_inc(s["added"], 1)
                    dve.wait_ge(s["added"], NCH * NT + 1)
                if l == 3:
                    break
                if l == 0:
                    dve.sem_inc(st[1]["sums_done"], 1)
                s = st[l + 1]

                def inverse(c, q, n):
                    dve.wait_ge(s["degree_ready"], c + 1)
                    to = acc[:, 1, cols(c, n)]
                    nc.vector.reciprocal(to, to).then_inc(s["inverse_ready"], 1)

                def average(c, q, n):
                    if l == 0:
                        dve.wait_ge(s["inverse_ready"], c + 1)
                    to = acc[:, 0, cols(c, n)]
                    nc.vector.tensor_tensor(to, to, acc[:, 1, cols(c, n)], ALU.mult).then_inc(s["agg_ready"], 1)

                def add_input(c, q, n):
                    dve.wait_ge(s["z_ready"], c + 1)
                    to = hT[:, cols(c, n)]
                    nc.vector.tensor_tensor(to, z[:, q, 0:n * P], to, ALU.add).then_inc(s["res_ready"], 1)

                def residual(c, q, n):
                    dve.wait_ge(s["turned"], c + 1)
                    dve.wait_ge(x_in[q], 16 * (c // 2) + 16)
                    nc.vector.tensor_tensor(kept(c, n), xin[:, q, 0:n], by_tile(2 + q, n), ALU.add).then_inc(s["x1_ready"], 1)
                    dve.wait_ge(s["x1_ready"], c + 1)

                def scale_and_shift(c, q, n):
                    dve.wait_ge(s["std_ready"], c + 1)
                    after(dve, s["hn_ready"], c - 1)
                    nc.vector.reciprocal(rstd[:, q, 0:n], std[:, q, 0:n]).then_inc(s["rstd_ready"], 1)
                    dve.wait_ge(s["rstd_ready"], c + 1)
                    nc.vector.scalar_tensor_tensor(out=shift[:, q, 0:n], in0=meanvar[:, q, 0:n, 0], scalar=-1.0, in1=rstd[:, q, 0:n],
                                                   op0=ALU.mult, op1=ALU.mult).then_inc(s["y_ready"], 1)

                def with_bias(c, q, n):
                    dve.wait_ge(s["row_mm"], c + 1)
                    after(dve, table_in[3][q], 16 * (c // 2))
                    nc.vector.tensor_tensor(rows[:, q, 0:n], by_tile(6 + q, n), mb1_all[:, :, :].to_broadcast([P, n, D]),
                                            ALU.add).then_inc(s["rows_ready"], 1)

                if l == 0:
                    staggered((1, average), (0, inverse))
                elif l == 1:
                    staggered((5, first_rest(s, rows_rows, hn)), (3, add_input), (0, average))
                else:
                    staggered((12, with_bias), (8, scale_and_shift), (6, statistics(s, residual)), (0, average))
            s = st[4]

            def result(c, q, n):
                dve.wait_ge(s["row_mm"], c + 1)
                dve.wait_ge(st[3]["ub2_added"], c + 1)
                after(dve, out_written[q], 16 * (c // 2))
                nc.vector.tensor_tensor(rows[:, q, 0:n], by_tile(2 + q, n), kept(c, n), ALU.add).then_inc(s["rows_ready"], 1)

            staggered((0, result))


def kernel(**inputs):
    import numpy as np
    import concourse.bacc as bacc
    from concourse.bass_utils import run_bass_kernel_spmd

    a = {k: np.asarray(v) for k, v in inputs.items()}
    src = np.concatenate([a["src"], np.zeros((FULL + 1) * BODY * P - E, a["src"].dtype)])
    dst = np.concatenate([a["dst"], np.full(EP - E, PAD_DST, a["dst"].dtype)])
    edge_T = np.zeros((D, EP), a["edge_attr_128"].dtype)
    edge_T[:, :E] = a["edge_attr_128"].T
    xp = np.zeros((NP, D), a["x"].dtype)
    xp[:N] = a["x"]
    arrays = {
        "x": xp,
        "src_t": np.ascontiguousarray(src.reshape(-1, P).T),
        "dst_t": np.ascontiguousarray(dst.reshape(NT, P).T),
        "dst_first": np.ascontiguousarray(dst[::BT * P].reshape(1, NB)),
        "edge_T": edge_T,
        "WlT": np.ascontiguousarray(np.stack([a[f"L0_gnn_W_l{k}"].T for k in (1, 2, 3)], axis=1)),
        "bl": np.stack([a[f"L0_gnn_b_l{k}"] for k in (1, 2, 3)]),
        "WrT": np.ascontiguousarray(np.stack([a[f"L0_gnn_W_r{k}"].T for k in (1, 2, 3)], axis=1)),
        "mw1": a["L1_gnn_mw1"], "mb1": a["L1_gnn_mb1"], "uw1": a["L1_gnn_uw1"], "ub1": a["L1_gnn_ub1"],
        "uw2": a["L1_gnn_uw2"], "ub2": a["L1_gnn_ub2"],
    }
    nc = bacc.Bacc("TRN2", target_bir_lowering=False, num_devices=1)
    args = [nc.dram_tensor(f"in_{n}", v.shape, mybir.dt.from_np(v.dtype), kind="ExternalInput").ap() for n, v in arrays.items()]
    out = nc.dram_tensor("out", (NP, D), F32, kind="ExternalOutput").ap()
    gnn_kernel(nc, *args, out)
    r = run_bass_kernel_spmd(nc, [{f"in_{n}": v for n, v in arrays.items()}], core_ids=[0])
    return r.results[0]["out"][:N]
```
